# Optimizing a Trainium2 kernel written in Bass

```python
import numpy as np
import jax
import jax.numpy as jnp

def _softmax(x, axis=-1):
    return jax.nn.softmax(x, axis=axis)

def _gelu(x):
    return jax.nn.gelu(x, approximate=True)

def _silu(x):
    return jax.nn.silu(x)

def _sigmoid(x):
    return jax.nn.sigmoid(x)

def _layernorm(x, axis=-1, eps=1e-05):
    m = jnp.mean(x, axis=axis, keepdims=True)
    v = jnp.var(x, axis=axis, keepdims=True)
    return (x - m) / jnp.sqrt(v + eps)

def _scatter_add(tgt, idx, src, axis=0):
    return tgt.at[idx].add(src)

def _segment_sum(src, seg, n):
    return jax.ops.segment_sum(src, seg, n)
kernel_name = 'mk_pixart_seq_d4_seqx_r8_4813fb'

def setup_inputs(seed: int=0):
    np.random.seed(seed)
    _w = jnp.asarray

    def _rec_inputs():
        import jax
        import jax.numpy as jnp
        _rk = jax.random.key(seed)
        x = -0.0005207 + 1.001 * jax.random.normal(jax.random.fold_in(_rk, 1), (16, 128, 128), jnp.float32)
        _lenS = 128 - jax.random.randint(jax.random.fold_in(_rk, 7), (16,), 0, max(1, 128 // 4) + 1, jnp.int32)
        _lenS2 = 128 - jax.random.randint(jax.random.fold_in(_rk, 8), (16,), 0, max(1, 128 // 4) + 1, jnp.int32)
        cond_1024 = 0.000887014 + 1.03683 * jax.random.normal(jax.random.fold_in(_rk, 11), (16, 128), jnp.float32)
        _ctx_768P = jax.random.normal(jax.random.fold_in(_rk, 12), (16, 16, 96), jnp.float32)
        _ctx_768c = jax.random.dirichlet(jax.random.fold_in(_rk, 512), 0.3 * jnp.ones((16,), jnp.float32), (16, 128))
        _ctx_768t = jnp.einsum('bsk,bkd->bsd', _ctx_768c, _ctx_768P)
        _ctx_768t = _ctx_768t * jax.lax.rsqrt(jnp.mean(jnp.square(_ctx_768t)) + 1e-12) * 0.953939
        ctx_768 = 0.000599585 + 1.00006 * (_ctx_768t + 0.3 * jax.random.normal(jax.random.fold_in(_rk, 612), (16, 128, 96), jnp.float32))
        return (x, cond_1024, ctx_768)
    x, cond_1024, ctx_768 = _rec_inputs()

    def _L0_xcond_setup():
        import jax, jax.numpy as jnp
        import numpy as np
        B, N, M = (2, 128, 64)
        D, H, DH = (128, 16, 64)
        MID = H * DH
        DC = 96
        MULT = 4
        EPS = 1e-05

        def _ln(x, w, b):
            mu = jnp.mean(x, -1, keepdims=True)
            var = jnp.mean((x - mu) ** 2, -1, keepdims=True)
            return (x - mu) * jax.lax.rsqrt(var + EPS) * w + b

        def _sincos(n, d):
            inv = 1.0 / 10000.0 ** (jnp.arange(0, d, 2, dtype=jnp.float32) / d)
            ang = jnp.arange(n, dtype=jnp.float32)[:, None] * inv[None, :]
            return (jnp.sin(ang), jnp.cos(ang))

        def _rope(x, sin, cos):
            s = sin[None, None]
            c = cos[None, None]
            xe = x[..., ::2]
            xo = x[..., 1::2]
            re = xe * c - xo * s
            ro = xe * s + xo * c
            return jnp.stack((re, ro), axis=-1).reshape(x.shape)

        def _heads(t):
            b, n, _ = t.shape
            return t.reshape(b, n, H, DH).transpose(0, 2, 1, 3)

        def _attn(xq, ctx, wq, wkv, wo, bo):
            q = _heads(xq @ wq)
            k, v = jnp.split(ctx @ wkv, 2, axis=-1)
            k = _heads(k)
            v = _heads(v)
            sq, cq = _sincos(q.shape[2], DH)
            sk, ck = _sincos(k.shape[2], DH)
            q = _rope(q, sq, cq)
            k = _rope(k, sk, ck)
            sim = jnp.einsum('bhnd,bhmd->bhnm', q, k) * DH ** (-0.5)
            a = jax.nn.softmax(sim, axis=-1)
            o = jnp.einsum('bhnm,bhmd->bhnd', a, v)
            o = o.transpose(0, 2, 1, 3).reshape(xq.shape[0], xq.shape[1], MID)
            return o @ wo + bo

        def _adaln(x, c, lw, lb, gw, gb, bw, bb):
            g = (c @ gw + gb)[:, None, :]
            bt = (c @ bw + bb)[:, None, :]
            return _ln(x, lw, lb) * (1.0 + g) + bt
        ks = jax.random.split(jax.random.key(seed), 24)
        s = 0.02
        inp = {'x': jax.random.normal(ks[0], (B, N, D), jnp.float32), 'cond': jax.random.normal(ks[1], (B, D), jnp.float32), 'context': jax.random.normal(ks[2], (B, M, DC), jnp.float32), 'ln1_w': jnp.ones((D,), jnp.float32), 'ln1_b': jnp.zeros((D,), jnp.float32), 'g1_w': jax.random.normal(ks[3], (D, D), jnp.float32) * s, 'g1_b': jnp.zeros((D,), jnp.float32), 'b1_w': jax.random.normal(ks[4], (D, D), jnp.float32) * s, 'b1_b': jnp.zeros((D,), jnp.float32), 'ln2_w': jnp.ones((D,), jnp.float32), 'ln2_b': jnp.zeros((D,), jnp.float32), 'g2_w': jax.random.normal(ks[5], (D, D), jnp.float32) * s, 'g2_b': jnp.zeros((D,), jnp.float32), 'b2_w': jax.random.normal(ks[6], (D, D), jnp.float32) * s, 'b2_b': jnp.zeros((D,), jnp.float32), 'sa_wq': jax.random.normal(ks[7], (D, MID), jnp.float32) * s, 'sa_wkv': jax.random.normal(ks[8], (D, 2 * MID), jnp.float32) * s, 'sa_wo': jax.random.normal(ks[9], (MID, D), jnp.float32) * s, 'sa_bo': jnp.zeros((D,), jnp.float32), 'ca_lnc_w': jnp.ones((DC,), jnp.float32), 'ca_lnc_b': jnp.zeros((DC,), jnp.float32), 'ca_wq': jax.random.normal(ks[10], (D, MID), jnp.float32) * s, 'ca_wkv': jax.random.normal(ks[11], (DC, 2 * MID), jnp.float32) * s, 'ca_wo': jax.random.normal(ks[12], (MID, D), jnp.float32) * s, 'ca_bo': jnp.zeros((D,), jnp.float32), 'ff_w1': jax.random.normal(ks[13], (D, MULT * D), jnp.float32) * s, 'ff_b1': jnp.zeros((MULT * D,), jnp.float32), 'ff_w2': jax.random.normal(ks[14], (MULT * D, D), jnp.float32) * s, 'ff_b2': jnp.zeros((D,), jnp.float32)}
        return inp
    _L0_xcond_all = _L0_xcond_setup()
    _L0_xcond_in = {k: v for k, v in _L0_xcond_all.items() if k in ('ln1_w', 'ln1_b', 'g1_w', 'g1_b', 'b1_w', 'b1_b', 'ln2_w', 'ln2_b', 'g2_w', 'g2_b', 'b2_w', 'b2_b', 'sa_wq', 'sa_wkv', 'sa_wo', 'sa_bo', 'ca_lnc_w', 'ca_lnc_b', 'ca_wq', 'ca_wkv', 'ca_wo', 'ca_bo', 'ff_w1', 'ff_b1', 'ff_w2', 'ff_b2')}
    del _L0_xcond_all

    def _L1_xcond_setup():
        import jax, jax.numpy as jnp
        import numpy as np
        B, N, D, H, TD, TL = (4, 128, 128, 16, 96, 77)
        HD = D // H
        EPS = 1e-06

        def _ln(x):
            mu = jnp.mean(x, axis=-1, keepdims=True)
            var = jnp.var(x, axis=-1, keepdims=True)
            return (x - mu) * jax.lax.rsqrt(var + EPS)

        def _modulate(x, shift, scale):
            return x * (1.0 + scale[:, None, :]) + shift[:, None, :]

        def _heads(t):
            return t.reshape(t.shape[0], t.shape[1], H, HD).transpose(0, 2, 1, 3)

        def _attend(q, k, v):
            sim = jnp.einsum('bhid,bhjd->bhij', q, k) * HD ** (-0.5)
            attn = jax.nn.softmax(sim, axis=-1)
            out = jnp.einsum('bhij,bhjd->bhid', attn, v)
            return out.transpose(0, 2, 1, 3).reshape(out.shape[0], -1, D)
        key = jax.random.key(seed)
        ks = jax.random.split(key, 16)
        s = 0.02
        return {'x': jax.random.normal(ks[0], (B, N, D), jnp.float32), 'c': jax.random.normal(ks[1], (B, D), jnp.float32), 'text_embed': jax.random.normal(ks[2], (B, TL, TD), jnp.float32), 'W_ada': jax.random.normal(ks[3], (D, 6 * D), jnp.float32) * s, 'b_ada': jnp.zeros((6 * D,), jnp.float32), 'W_qkv': jax.random.normal(ks[4], (D, 3 * D), jnp.float32) * s, 'b_qkv': jnp.zeros((3 * D,), jnp.float32), 'W_proj': jax.random.normal(ks[5], (D, D), jnp.float32) * s, 'b_proj': jnp.zeros((D,), jnp.float32), 'W_ctx': jax.random.normal(ks[6], (TD, D), jnp.float32) * s, 'b_ctx': jnp.zeros((D,), jnp.float32), 'W_q': jax.random.normal(ks[7], (D, D), jnp.float32) * s, 'W_k': jax.random.normal(ks[8], (D, D), jnp.float32) * s, 'W_v': jax.random.normal(ks[9], (D, D), jnp.float32) * s, 'W_out': jax.random.normal(ks[10], (D, D), jnp.float32) * s, 'b_out': jnp.zeros((D,), jnp.float32), 'W_fc1': jax.random.normal(ks[11], (D, 4 * D), jnp.float32) * s, 'b_fc1': jnp.zeros((4 * D,), jnp.float32), 'W_fc2': jax.random.normal(ks[12], (4 * D, D), jnp.float32) * s, 'b_fc2': jnp.zeros((D,), jnp.float32)}
    _L1_xcond_all = _L1_xcond_setup()
    _L1_xcond_in = {k: v for k, v in _L1_xcond_all.items() if k in ('W_ada', 'b_ada', 'W_qkv', 'b_qkv', 'W_proj', 'b_proj', 'W_ctx', 'b_ctx', 'W_q', 'W_k', 'W_v', 'W_out', 'b_out', 'W_fc1', 'b_fc1', 'W_fc2', 'b_fc2')}
    del _L1_xcond_all

    def _L2_xcond_setup():
        import jax, jax.numpy as jnp
        import numpy as np
        EPS = 1e-05

        def _ada_ln(x, t, W, b):
            emb = t @ W + b
            scale, shift = jnp.split(emb, 2, axis=-1)
            mu = x.mean(-1, keepdims=True)
            var = ((x - mu) ** 2).mean(-1, keepdims=True)
            xn = (x - mu) * jax.lax.rsqrt(var + EPS)
            return xn * (1.0 + scale) + shift

        def _attn(x, ctx, Wq, Wk, Wv, Wo, bo, heads):
            b, n, _ = x.shape
            j = ctx.shape[1]
            q = (x @ Wq).reshape(b, n, heads, -1)
            k = (ctx @ Wk).reshape(b, j, heads, -1)
            v = (ctx @ Wv).reshape(b, j, heads, -1)
            scale = q.shape[-1] ** (-0.5)
            sim = jnp.einsum('bihd,bjhd->bhij', q, k) * scale
            attn = jax.nn.softmax(sim, axis=-1)
            out = jnp.einsum('bhij,bjhd->bihd', attn, v).reshape(b, n, -1)
            return out @ Wo + bo

        def _ff(x, W1, b1, W2, b2):
            p = x @ W1 + b1
            a, gate = jnp.split(p, 2, axis=-1)
            return a * jax.nn.gelu(gate, approximate=False) @ W2 + b2
        key = jax.random.key(seed)
        ks = jax.random.split(key, 32)
        B, N, D = (4, 256, 128)
        J, CD = (32, 96)
        H, DH = (16, 64)
        INNER = H * DH
        FF = 4 * D
        w = lambda k, shp: jax.random.normal(k, shp, jnp.float32) * 0.02
        inp = {'x': jax.random.normal(ks[0], (B, N, D), jnp.float32), 't': jax.random.normal(ks[1], (B, 1, D), jnp.float32), 'context': jax.random.normal(ks[2], (B, J, CD), jnp.float32), 'n1_w': w(ks[3], (D, 2 * D)), 'n1_b': jnp.zeros((2 * D,), jnp.float32), 'n2_w': w(ks[4], (D, 2 * D)), 'n2_b': jnp.zeros((2 * D,), jnp.float32), 'n3_w': w(ks[5], (D, 2 * D)), 'n3_b': jnp.zeros((2 * D,), jnp.float32), 'q1': w(ks[6], (D, INNER)), 'k1': w(ks[7], (D, INNER)), 'v1': w(ks[8], (D, INNER)), 'o1_w': w(ks[9], (INNER, D)), 'o1_b': jnp.zeros((D,), jnp.float32), 'q2': w(ks[10], (D, INNER)), 'k2': w(ks[11], (CD, INNER)), 'v2': w(ks[12], (CD, INNER)), 'o2_w': w(ks[13], (INNER, D)), 'o2_b': jnp.zeros((D,), jnp.float32), 'ff_w1': w(ks[14], (D, 2 * FF)), 'ff_b1': jnp.zeros((2 * FF,), jnp.float32), 'ff_w2': w(ks[15], (FF, D)), 'ff_b2': jnp.zeros((D,), jnp.float32)}
        return inp
    _L2_xcond_all = _L2_xcond_setup()
    _L2_xcond_in = {k: v for k, v in _L2_xcond_all.items() if k in ('n1_w', 'n1_b', 'n2_w', 'n2_b', 'n3_w', 'n3_b', 'q1', 'k1', 'v1', 'o1_w', 'o1_b', 'q2', 'k2', 'v2', 'o2_w', 'o2_b', 'ff_w1', 'ff_b1', 'ff_w2', 'ff_b2')}
    del _L2_xcond_all

    def _L3_xcond_setup():
        import jax, jax.numpy as jnp
        import numpy as np
        EPS = 1e-06

        def ln(x, eps=EPS):
            m = jnp.mean(x, axis=-1, keepdims=True)
            v = jnp.mean(jnp.square(x - m), axis=-1, keepdims=True)
            return (x - m) * jax.lax.rsqrt(v + eps)

        def modulate(x, shift, scale):
            return x * (1.0 + scale[:, None, :]) + shift[:, None, :]

        def _heads(t, H):
            B, N, D = t.shape
            return t.reshape(B, N, H, D // H).transpose(0, 2, 1, 3)

        def _unheads(t):
            B, H, N, hd = t.shape
            return t.transpose(0, 2, 1, 3).reshape(B, N, H * hd)
        key = jax.random.key(seed)
        B, N, D, H, T, CD = (4, 128, 128, 16, 32, 96)
        FF = 4 * D
        ks = jax.random.split(key, 20)
        s = 0.02
        return {'x': jax.random.normal(ks[0], (B, N, D), jnp.float32), 'c': jax.random.normal(ks[1], (B, D), jnp.float32), 'brain_tokens': jax.random.normal(ks[2], (B, T, CD), jnp.float32), 'adaln_w': jax.random.normal(ks[3], (9 * D, D), jnp.float32) * s, 'adaln_b': jax.random.normal(ks[4], (9 * D,), jnp.float32) * s, 'qn_w': jnp.ones((D // H,), jnp.float32), 'qn_b': jnp.zeros((D // H,), jnp.float32), 'kn_w': jnp.ones((D // H,), jnp.float32), 'kn_b': jnp.zeros((D // H,), jnp.float32), 'ca_in_w': jax.random.normal(ks[5], (3 * D, D), jnp.float32) * s, 'ca_in_b': jax.random.normal(ks[6], (3 * D,), jnp.float32) * s, 'ca_out_w': jax.random.normal(ks[7], (D, D), jnp.float32) * s, 'ca_out_b': jax.random.normal(ks[8], (D,), jnp.float32) * s, 'cond_w': jax.random.normal(ks[9], (D, CD), jnp.float32) * s, 'cond_b': jax.random.normal(ks[10], (D,), jnp.float32) * s, 'w1': jax.random.normal(ks[11], (FF, D), jnp.float32) * s, 'w3': jax.random.normal(ks[12], (FF, D), jnp.float32) * s, 'w2': jax.random.normal(ks[13], (D, FF), jnp.float32) * s}
    _L3_xcond_all = _L3_xcond_setup()
    _L3_xcond_in = {k: v for k, v in _L3_xcond_all.items() if k in ('adaln_w', 'adaln_b', 'qn_w', 'qn_b', 'kn_w', 'kn_b', 'ca_in_w', 'ca_in_b', 'ca_out_w', 'ca_out_b', 'cond_w', 'cond_b', 'w1', 'w3', 'w2')}
    del _L3_xcond_all
    return {'x': x, 'cond_1024': cond_1024, 'ctx_768': ctx_768, 'L0_xcond_ln1_w': _L0_xcond_in['ln1_w'], 'L0_xcond_ln1_b': _L0_xcond_in['ln1_b'], 'L0_xcond_g1_w': _L0_xcond_in['g1_w'], 'L0_xcond_g1_b': _L0_xcond_in['g1_b'], 'L0_xcond_b1_w': _L0_xcond_in['b1_w'], 'L0_xcond_b1_b': _L0_xcond_in['b1_b'], 'L0_xcond_ln2_w': _L0_xcond_in['ln2_w'], 'L0_xcond_ln2_b': _L0_xcond_in['ln2_b'], 'L0_xcond_g2_w': _L0_xcond_in['g2_w'], 'L0_xcond_g2_b': _L0_xcond_in['g2_b'], 'L0_xcond_b2_w': _L0_xcond_in['b2_w'], 'L0_xcond_b2_b': _L0_xcond_in['b2_b'], 'L0_xcond_sa_wq': _L0_xcond_in['sa_wq'], 'L0_xcond_sa_wkv': _L0_xcond_in['sa_wkv'], 'L0_xcond_sa_wo': _L0_xcond_in['sa_wo'], 'L0_xcond_sa_bo': _L0_xcond_in['sa_bo'], 'L0_xcond_ca_lnc_w': _L0_xcond_in['ca_lnc_w'], 'L0_xcond_ca_lnc_b': _L0_xcond_in['ca_lnc_b'], 'L0_xcond_ca_wq': _L0_xcond_in['ca_wq'], 'L0_xcond_ca_wkv': _L0_xcond_in['ca_wkv'], 'L0_xcond_ca_wo': _L0_xcond_in['ca_wo'], 'L0_xcond_ca_bo': _L0_xcond_in['ca_bo'], 'L0_xcond_ff_w1': _L0_xcond_in['ff_w1'], 'L0_xcond_ff_b1': _L0_xcond_in['ff_b1'], 'L0_xcond_ff_w2': _L0_xcond_in['ff_w2'], 'L0_xcond_ff_b2': _L0_xcond_in['ff_b2'], 'L1_xcond_W_ada': _L1_xcond_in['W_ada'], 'L1_xcond_b_ada': _L1_xcond_in['b_ada'], 'L1_xcond_W_qkv': _L1_xcond_in['W_qkv'], 'L1_xcond_b_qkv': _L1_xcond_in['b_qkv'], 'L1_xcond_W_proj': _L1_xcond_in['W_proj'], 'L1_xcond_b_proj': _L1_xcond_in['b_proj'], 'L1_xcond_W_ctx': _L1_xcond_in['W_ctx'], 'L1_xcond_b_ctx': _L1_xcond_in['b_ctx'], 'L1_xcond_W_q': _L1_xcond_in['W_q'], 'L1_xcond_W_k': _L1_xcond_in['W_k'], 'L1_xcond_W_v': _L1_xcond_in['W_v'], 'L1_xcond_W_out': _L1_xcond_in['W_out'], 'L1_xcond_b_out': _L1_xcond_in['b_out'], 'L1_xcond_W_fc1': _L1_xcond_in['W_fc1'], 'L1_xcond_b_fc1': _L1_xcond_in['b_fc1'], 'L1_xcond_W_fc2': _L1_xcond_in['W_fc2'], 'L1_xcond_b_fc2': _L1_xcond_in['b_fc2'], 'L2_xcond_n1_w': _L2_xcond_in['n1_w'], 'L2_xcond_n1_b': _L2_xcond_in['n1_b'], 'L2_xcond_n2_w': _L2_xcond_in['n2_w'], 'L2_xcond_n2_b': _L2_xcond_in['n2_b'], 'L2_xcond_n3_w': _L2_xcond_in['n3_w'], 'L2_xcond_n3_b': _L2_xcond_in['n3_b'], 'L2_xcond_q1': _L2_xcond_in['q1'], 'L2_xcond_k1': _L2_xcond_in['k1'], 'L2_xcond_v1': _L2_xcond_in['v1'], 'L2_xcond_o1_w': _L2_xcond_in['o1_w'], 'L2_xcond_o1_b': _L2_xcond_in['o1_b'], 'L2_xcond_q2': _L2_xcond_in['q2'], 'L2_xcond_k2': _L2_xcond_in['k2'], 'L2_xcond_v2': _L2_xcond_in['v2'], 'L2_xcond_o2_w': _L2_xcond_in['o2_w'], 'L2_xcond_o2_b': _L2_xcond_in['o2_b'], 'L2_xcond_ff_w1': _L2_xcond_in['ff_w1'], 'L2_xcond_ff_b1': _L2_xcond_in['ff_b1'], 'L2_xcond_ff_w2': _L2_xcond_in['ff_w2'], 'L2_xcond_ff_b2': _L2_xcond_in['ff_b2'], 'L3_xcond_adaln_w': _L3_xcond_in['adaln_w'], 'L3_xcond_adaln_b': _L3_xcond_in['adaln_b'], 'L3_xcond_qn_w': _L3_xcond_in['qn_w'], 'L3_xcond_qn_b': _L3_xcond_in['qn_b'], 'L3_xcond_kn_w': _L3_xcond_in['kn_w'], 'L3_xcond_kn_b': _L3_xcond_in['kn_b'], 'L3_xcond_ca_in_w': _L3_xcond_in['ca_in_w'], 'L3_xcond_ca_in_b': _L3_xcond_in['ca_in_b'], 'L3_xcond_ca_out_w': _L3_xcond_in['ca_out_w'], 'L3_xcond_ca_out_b': _L3_xcond_in['ca_out_b'], 'L3_xcond_cond_w': _L3_xcond_in['cond_w'], 'L3_xcond_cond_b': _L3_xcond_in['cond_b'], 'L3_xcond_w1': _L3_xcond_in['w1'], 'L3_xcond_w3': _L3_xcond_in['w3'], 'L3_xcond_w2': _L3_xcond_in['w2']}

def reference(x, cond_1024, ctx_768, L0_xcond_ln1_w, L0_xcond_ln1_b, L0_xcond_g1_w, L0_xcond_g1_b, L0_xcond_b1_w, L0_xcond_b1_b, L0_xcond_ln2_w, L0_xcond_ln2_b, L0_xcond_g2_w, L0_xcond_g2_b, L0_xcond_b2_w, L0_xcond_b2_b, L0_xcond_sa_wq, L0_xcond_sa_wkv, L0_xcond_sa_wo, L0_xcond_sa_bo, L0_xcond_ca_lnc_w, L0_xcond_ca_lnc_b, L0_xcond_ca_wq, L0_xcond_ca_wkv, L0_xcond_ca_wo, L0_xcond_ca_bo, L0_xcond_ff_w1, L0_xcond_ff_b1, L0_xcond_ff_w2, L0_xcond_ff_b2, L1_xcond_W_ada, L1_xcond_b_ada, L1_xcond_W_qkv, L1_xcond_b_qkv, L1_xcond_W_proj, L1_xcond_b_proj, L1_xcond_W_ctx, L1_xcond_b_ctx, L1_xcond_W_q, L1_xcond_W_k, L1_xcond_W_v, L1_xcond_W_out, L1_xcond_b_out, L1_xcond_W_fc1, L1_xcond_b_fc1, L1_xcond_W_fc2, L1_xcond_b_fc2, L2_xcond_n1_w, L2_xcond_n1_b, L2_xcond_n2_w, L2_xcond_n2_b, L2_xcond_n3_w, L2_xcond_n3_b, L2_xcond_q1, L2_xcond_k1, L2_xcond_v1, L2_xcond_o1_w, L2_xcond_o1_b, L2_xcond_q2, L2_xcond_k2, L2_xcond_v2, L2_xcond_o2_w, L2_xcond_o2_b, L2_xcond_ff_w1, L2_xcond_ff_b1, L2_xcond_ff_w2, L2_xcond_ff_b2, L3_xcond_adaln_w, L3_xcond_adaln_b, L3_xcond_qn_w, L3_xcond_qn_b, L3_xcond_kn_w, L3_xcond_kn_b, L3_xcond_ca_in_w, L3_xcond_ca_in_b, L3_xcond_ca_out_w, L3_xcond_ca_out_b, L3_xcond_cond_w, L3_xcond_cond_b, L3_xcond_w1, L3_xcond_w3, L3_xcond_w2):
    import jax
    import jax.numpy as jnp

    def _L0_xcond_ref(x, cond, context, ln1_w, ln1_b, g1_w, g1_b, b1_w, b1_b, ln2_w, ln2_b, g2_w, g2_b, b2_w, b2_b, sa_wq, sa_wkv, sa_wo, sa_bo, ca_lnc_w, ca_lnc_b, ca_wq, ca_wkv, ca_wo, ca_bo, ff_w1, ff_b1, ff_w2, ff_b2):
        import jax, jax.numpy as jnp
        import numpy as np
        B, N, M = (2, 128, 64)
        D, H, DH = (128, 16, 64)
        MID = H * DH
        DC = 96
        MULT = 4
        EPS = 1e-05

        def _ln(x, w, b):
            mu = jnp.mean(x, -1, keepdims=True)
            var = jnp.mean((x - mu) ** 2, -1, keepdims=True)
            return (x - mu) * jax.lax.rsqrt(var + EPS) * w + b

        def _sincos(n, d):
            inv = 1.0 / 10000.0 ** (jnp.arange(0, d, 2, dtype=jnp.float32) / d)
            ang = jnp.arange(n, dtype=jnp.float32)[:, None] * inv[None, :]
            return (jnp.sin(ang), jnp.cos(ang))

        def _rope(x, sin, cos):
            s = sin[None, None]
            c = cos[None, None]
            xe = x[..., ::2]
            xo = x[..., 1::2]
            re = xe * c - xo * s
            ro = xe * s + xo * c
            return jnp.stack((re, ro), axis=-1).reshape(x.shape)

        def _heads(t):
            b, n, _ = t.shape
            return t.reshape(b, n, H, DH).transpose(0, 2, 1, 3)

        def _attn(xq, ctx, wq, wkv, wo, bo):
            q = _heads(xq @ wq)
            k, v = jnp.split(ctx @ wkv, 2, axis=-1)
            k = _heads(k)
            v = _heads(v)
            sq, cq = _sincos(q.shape[2], DH)
            sk, ck = _sincos(k.shape[2], DH)
            q = _rope(q, sq, cq)
            k = _rope(k, sk, ck)
            sim = jnp.einsum('bhnd,bhmd->bhnm', q, k) * DH ** (-0.5)
            a = jax.nn.softmax(sim, axis=-1)
            o = jnp.einsum('bhnm,bhmd->bhnd', a, v)
            o = o.transpose(0, 2, 1, 3).reshape(xq.shape[0], xq.shape[1], MID)
            return o @ wo + bo

        def _adaln(x, c, lw, lb, gw, gb, bw, bb):
            g = (c @ gw + gb)[:, None, :]
            bt = (c @ bw + bb)[:, None, :]
            return _ln(x, lw, lb) * (1.0 + g) + bt
        attn_in = _adaln(x, cond, ln1_w, ln1_b, g1_w, g1_b, b1_w, b1_b)
        x = _attn(attn_in, attn_in, sa_wq, sa_wkv, sa_wo, sa_bo) + x
        cross_in = _adaln(x, cond, ln1_w, ln1_b, g1_w, g1_b, b1_w, b1_b)
        ctx_n = _ln(context, ca_lnc_w, ca_lnc_b)
        x = _attn(cross_in, ctx_n, ca_wq, ca_wkv, ca_wo, ca_bo) + x
        ffn_in = _adaln(x, cond, ln2_w, ln2_b, g2_w, g2_b, b2_w, b2_b)
        h = jax.nn.gelu(ffn_in @ ff_w1 + ff_b1, approximate=False)
        x = h @ ff_w2 + ff_b2 + x
        return x

    def _L1_xcond_ref(x, c, text_embed, W_ada, b_ada, W_qkv, b_qkv, W_proj, b_proj, W_ctx, b_ctx, W_q, W_k, W_v, W_out, b_out, W_fc1, b_fc1, W_fc2, b_fc2):
        import jax, jax.numpy as jnp
        import numpy as np
        B, N, D, H, TD, TL = (4, 128, 128, 16, 96, 77)
        HD = D // H
        EPS = 1e-06

        def _ln(x):
            mu = jnp.mean(x, axis=-1, keepdims=True)
            var = jnp.var(x, axis=-1, keepdims=True)
            return (x - mu) * jax.lax.rsqrt(var + EPS)

        def _modulate(x, shift, scale):
            return x * (1.0 + scale[:, None, :]) + shift[:, None, :]

        def _heads(t):
            return t.reshape(t.shape[0], t.shape[1], H, HD).transpose(0, 2, 1, 3)

        def _attend(q, k, v):
            sim = jnp.einsum('bhid,bhjd->bhij', q, k) * HD ** (-0.5)
            attn = jax.nn.softmax(sim, axis=-1)
            out = jnp.einsum('bhij,bhjd->bhid', attn, v)
            return out.transpose(0, 2, 1, 3).reshape(out.shape[0], -1, D)
        mod = jax.nn.silu(c) @ W_ada + b_ada
        sh_msa, sc_msa, sh_x, sc_x, sh_mlp, sc_mlp = jnp.split(mod, 6, axis=-1)
        h1 = _modulate(_ln(x), sh_msa, sc_msa)
        qkv = h1 @ W_qkv + b_qkv
        q, k, v = jnp.split(qkv, 3, axis=-1)
        out = _attend(_heads(q), _heads(k), _heads(v))
        x = x + (out @ W_proj + b_proj)
        h2 = _modulate(_ln(x), sh_x, sc_x)
        ctx = text_embed @ W_ctx + b_ctx
        q = _heads(h2 @ W_q)
        k = _heads(ctx @ W_k)
        v = _heads(ctx @ W_v)
        out = _attend(q, k, v)
        x = x + (out @ W_out + b_out)
        h3 = _modulate(_ln(x), sh_mlp, sc_mlp)
        hidden = jax.nn.gelu(h3 @ W_fc1 + b_fc1, approximate=True)
        x = x + (hidden @ W_fc2 + b_fc2)
        return x

    def _L2_xcond_ref(x, t, context, n1_w, n1_b, n2_w, n2_b, n3_w, n3_b, q1, k1, v1, o1_w, o1_b, q2, k2, v2, o2_w, o2_b, ff_w1, ff_b1, ff_w2, ff_b2):
        import jax, jax.numpy as jnp
        import numpy as np
        EPS = 1e-05

        def _ada_ln(x, t, W, b):
            emb = t @ W + b
            scale, shift = jnp.split(emb, 2, axis=-1)
            mu = x.mean(-1, keepdims=True)
            var = ((x - mu) ** 2).mean(-1, keepdims=True)
            xn = (x - mu) * jax.lax.rsqrt(var + EPS)
            return xn * (1.0 + scale) + shift

        def _attn(x, ctx, Wq, Wk, Wv, Wo, bo, heads):
            b, n, _ = x.shape
            j = ctx.shape[1]
            q = (x @ Wq).reshape(b, n, heads, -1)
            k = (ctx @ Wk).reshape(b, j, heads, -1)
            v = (ctx @ Wv).reshape(b, j, heads, -1)
            scale = q.shape[-1] ** (-0.5)
            sim = jnp.einsum('bihd,bjhd->bhij', q, k) * scale
            attn = jax.nn.softmax(sim, axis=-1)
            out = jnp.einsum('bhij,bjhd->bihd', attn, v).reshape(b, n, -1)
            return out @ Wo + bo

        def _ff(x, W1, b1, W2, b2):
            p = x @ W1 + b1
            a, gate = jnp.split(p, 2, axis=-1)
            return a * jax.nn.gelu(gate, approximate=False) @ W2 + b2
        H = 16
        h = _ada_ln(x, t, n1_w, n1_b)
        x = _attn(h, h, q1, k1, v1, o1_w, o1_b, H) + x
        h = _ada_ln(x, t, n2_w, n2_b)
        x = _attn(h, context, q2, k2, v2, o2_w, o2_b, H) + x
        h = _ada_ln(x, t, n3_w, n3_b)
        x = _ff(h, ff_w1, ff_b1, ff_w2, ff_b2) + x
        return x

    def _L3_xcond_ref(x, c, brain_tokens, adaln_w, adaln_b, qn_w, qn_b, kn_w, kn_b, ca_in_w, ca_in_b, ca_out_w, ca_out_b, cond_w, cond_b, w1, w3, w2):
        import jax, jax.numpy as jnp
        import numpy as np
        EPS = 1e-06

        def ln(x, eps=EPS):
            m = jnp.mean(x, axis=-1, keepdims=True)
            v = jnp.mean(jnp.square(x - m), axis=-1, keepdims=True)
            return (x - m) * jax.lax.rsqrt(v + eps)

        def modulate(x, shift, scale):
            return x * (1.0 + scale[:, None, :]) + shift[:, None, :]

        def _heads(t, H):
            B, N, D = t.shape
            return t.reshape(B, N, H, D // H).transpose(0, 2, 1, 3)

        def _unheads(t):
            B, H, N, hd = t.shape
            return t.transpose(0, 2, 1, 3).reshape(B, N, H * hd)
        B, N, D = x.shape
        H = 16
        hd = D // H
        scale = hd ** (-0.5)
        mod = jax.nn.silu(c) @ adaln_w.T + adaln_b
        shift_sa, scale_sa, gate_sa, shift_ca, scale_ca, gate_ca, shift_ff, scale_ff, gate_ff = jnp.split(mod, 9, axis=-1)
        h = modulate(ln(x), shift_sa, scale_sa)
        q = ln(_heads(h, H)) * qn_w + qn_b
        k = ln(_heads(h, H)) * kn_w + kn_b
        v = _heads(h, H)
        attn = jax.nn.softmax(jnp.einsum('bhqd,bhkd->bhqk', q, k) * scale, axis=-1)
        h = _unheads(jnp.einsum('bhqk,bhkd->bhqd', attn, v))
        x = x + gate_sa[:, None, :] * h
        h = modulate(ln(x), shift_ca, scale_ca)
        kv = brain_tokens @ cond_w.T + cond_b
        wq, wk, wv = jnp.split(ca_in_w, 3, axis=0)
        bq, bk, bv = jnp.split(ca_in_b, 3, axis=0)
        q = _heads(h @ wq.T + bq, H)
        k = _heads(kv @ wk.T + bk, H)
        v = _heads(kv @ wv.T + bv, H)
        attn = jax.nn.softmax(jnp.einsum('bhqd,bhkd->bhqk', q, k) * scale, axis=-1)
        h = _unheads(jnp.einsum('bhqk,bhkd->bhqd', attn, v)) @ ca_out_w.T + ca_out_b
        x = x + gate_ca[:, None, :] * h
        h = modulate(ln(x), shift_ff, scale_ff)
        h = jax.nn.silu(h @ w1.T) * (h @ w3.T) @ w2.T
        x = x + gate_ff[:, None, :] * h
        return x
    x = _L0_xcond_ref(x, cond_1024, ctx_768, L0_xcond_ln1_w, L0_xcond_ln1_b, L0_xcond_g1_w, L0_xcond_g1_b, L0_xcond_b1_w, L0_xcond_b1_b, L0_xcond_ln2_w, L0_xcond_ln2_b, L0_xcond_g2_w, L0_xcond_g2_b, L0_xcond_b2_w, L0_xcond_b2_b, L0_xcond_sa_wq, L0_xcond_sa_wkv, L0_xcond_sa_wo, L0_xcond_sa_bo, L0_xcond_ca_lnc_w, L0_xcond_ca_lnc_b, L0_xcond_ca_wq, L0_xcond_ca_wkv, L0_xcond_ca_wo, L0_xcond_ca_bo, L0_xcond_ff_w1, L0_xcond_ff_b1, L0_xcond_ff_w2, L0_xcond_ff_b2)
    x = _L1_xcond_ref(x, cond_1024, ctx_768, L1_xcond_W_ada, L1_xcond_b_ada, L1_xcond_W_qkv, L1_xcond_b_qkv, L1_xcond_W_proj, L1_xcond_b_proj, L1_xcond_W_ctx, L1_xcond_b_ctx, L1_xcond_W_q, L1_xcond_W_k, L1_xcond_W_v, L1_xcond_W_out, L1_xcond_b_out, L1_xcond_W_fc1, L1_xcond_b_fc1, L1_xcond_W_fc2, L1_xcond_b_fc2)
    x = _L2_xcond_ref(x, cond_1024[:, None, :], ctx_768, L2_xcond_n1_w, L2_xcond_n1_b, L2_xcond_n2_w, L2_xcond_n2_b, L2_xcond_n3_w, L2_xcond_n3_b, L2_xcond_q1, L2_xcond_k1, L2_xcond_v1, L2_xcond_o1_w, L2_xcond_o1_b, L2_xcond_q2, L2_xcond_k2, L2_xcond_v2, L2_xcond_o2_w, L2_xcond_o2_b, L2_xcond_ff_w1, L2_xcond_ff_b1, L2_xcond_ff_w2, L2_xcond_ff_b2)
    x = _L3_xcond_ref(x, cond_1024, ctx_768, L3_xcond_adaln_w, L3_xcond_adaln_b, L3_xcond_qn_w, L3_xcond_qn_b, L3_xcond_kn_w, L3_xcond_kn_b, L3_xcond_ca_in_w, L3_xcond_ca_in_b, L3_xcond_ca_out_w, L3_xcond_ca_out_b, L3_xcond_cond_w, L3_xcond_cond_b, L3_xcond_w1, L3_xcond_w3, L3_xcond_w2)
    return x

_drawn_inputs = setup_inputs


def setup_inputs(seed=0):
    import zlib

    import numpy as np

    out = dict(_drawn_inputs(seed))
    spreads = {'L0_xcond_ln1_w': (1.0, 0.6),
     'L0_xcond_ln1_b': (0.0, 0.587),
     'L0_xcond_g1_b': (0.0, 0.8),
     'L0_xcond_b1_b': (0.0, 0.521),
     'L0_xcond_ln2_w': (1.0, 0.6),
     'L0_xcond_ln2_b': (0.0, 0.8),
     'L0_xcond_g2_b': (0.0, 0.8),
     'L0_xcond_b2_b': (0.0, 0.8),
     'L0_xcond_sa_bo': (0.0, 0.1),
     'L0_xcond_ca_lnc_w': (1.0, 0.6),
     'L0_xcond_ca_lnc_b': (0.0, 0.633),
     'L0_xcond_ca_bo': (0.0, 0.1),
     'L0_xcond_ff_b1': (0.0, 0.358),
     'L0_xcond_ff_b2': (0.0, 0.1),
     'L1_xcond_b_ada': (0.0, 0.8),
     'L1_xcond_b_qkv': (0.0, 0.346),
     'L1_xcond_b_proj': (0.0, 0.1),
     'L1_xcond_b_ctx': (0.0, 0.8),
     'L1_xcond_b_out': (0.0, 0.507),
     'L1_xcond_b_fc1': (0.0, 1.447),
     'L1_xcond_b_fc2': (0.0, 0.472),
     'L2_xcond_n1_b': (0.0, 2.0),
     'L2_xcond_n2_b': (0.0, 2.0),
     'L2_xcond_n3_b': (0.0, 0.8),
     'L2_xcond_o1_b': (0.0, 0.478),
     'L2_xcond_o2_b': (0.0, 0.47),
     'L2_xcond_ff_b1': (0.0, 0.8),
     'L2_xcond_ff_b2': (0.0, 0.8),
     'L3_xcond_qn_w': (1.0, 0.6),
     'L3_xcond_qn_b': (0.0, 2.0),
     'L3_xcond_kn_w': (1.0, 0.6),
     'L3_xcond_kn_b': (0.0, 2.0)}
    factors = {'L0_xcond_g1_w': 8.0,
     'L0_xcond_g2_w': 4.425,
     'L0_xcond_b2_w': 4.603,
     'L0_xcond_sa_wq': 8.0,
     'L0_xcond_ca_wq': 8.0,
     'L1_xcond_W_ada': 4.434,
     'L1_xcond_W_qkv': 4.068,
     'L1_xcond_W_ctx': 8.0,
     'L1_xcond_W_q': 8.0,
     'L1_xcond_W_k': 8.0,
     'L1_xcond_W_v': 7.626,
     'L1_xcond_W_out': 7.796,
     'L2_xcond_n2_w': 22.458,
     'L2_xcond_n3_w': 8.0,
     'L2_xcond_q1': 25.985,
     'L2_xcond_k1': 25.214,
     'L2_xcond_q2': 21.361,
     'L2_xcond_k2': 8.0,
     'L2_xcond_ff_w1': 3.679,
     'L2_xcond_ff_w2': 3.634,
     'L3_xcond_adaln_b': 5.352,
     'L3_xcond_ca_in_w': 8.0,
     'L3_xcond_ca_in_b': 30.629,
     'L3_xcond_ca_out_w': 8.0,
     'L3_xcond_ca_out_b': 64.0,
     'L3_xcond_cond_w': 8.0,
     'L3_xcond_cond_b': 42.981,
     'L3_xcond_w1': 8.0,
     'L3_xcond_w3': 8.0,
     'L3_xcond_w2': 8.0,
     'L1_xcond_W_fc1': 3.27,
     'L2_xcond_n1_w': 5.294}
    for name, (base, spread) in spreads.items():
        noise = np.random.default_rng([zlib.crc32(name.encode()), seed]).standard_normal(out[name].shape)
        drawn = base * np.exp(spread * noise) if base else spread * noise
        out[name] = jnp.asarray(drawn.astype(out[name].dtype))
    for name, factor in factors.items():
        out[name] = (out[name] * factor).astype(out[name].dtype)
    return out
```

```python
import concourse.bass as bass
from concourse import mybir
from contextlib import ExitStack
import numpy as np

S, N, D, CD = 16, 128, 128, 96
H, DH, HD = 16, 64, 8
MID = H * DH
PAIRS = S // 2
BANKS, BANK = 8, 512
T4 = 4

KIND = ["rope", "rope", "ff", "small", "small", "ff", "flat", "flat", "ff", "small", "small", "ff"]
CROSS = [False, True, False] * 4
LAST = len(KIND) - 1
EPS = [1e-5] * 3 + [1e-6] * 3 + [1e-5] * 3 + [1e-6] * 3
EPS_CTX = 1e-5
MODPAIR = [0, 0, 1, 2, 3, 4, 5, 6, 7, 8, 9, 10]
NMOD = 11
L3_SELF, L3_CROSS, L3_FF = 9, 10, 11
L2_FF = 8

VEC = {n: i for i, n in enumerate(
    ["ln1_w", "ln1_b", "ln2_w", "ln2_b"]
    + [f"raw{i}" for i in range(22)]
    + [f"ff1_0_{t}" for t in range(4)] + ["bq1", "bk1", "bctx"] + [f"fc1_{t}" for t in range(4)]
    + [f"ff1_2_{t}" for t in range(8)] + ["qn_w", "qn_b", "kn_w", "kn_b", "bq3", "bk3", "bcond"])}
ROW = {n: i for i, n in enumerate(
    ["o0", "o1", "o2", "o3", "o4", "o5", "o6", "o7", "o8", "o10", "bv1", "bv3", "g0", "g1", "g2"])}
OUT_ROW = ["o0", "o1", "o2", "o3", "o4", "o5", "o6", "o7", "o8", None, "o10", None]
CONST, _c = {}, 0
for _n, _w in [("ident", 128), ("center", 128), ("mean8", 128), ("rowmask", 4), ("colmask", 512),
               ("cosq", 64), ("sinq", 64), ("cosk", 64), ("sink", 64), ("neghalf", 1)]:
    CONST[_n] = slice(_c, _c + _w)
    _c += _w
NCONST = _c


def schedule():
    order = [("prelude", 0, 0), ("prelude", 0, 1)]
    for b in range(len(KIND)):
        before = [("scores", b - 1, 1)] if b else []
        order += [("project", b, 0)] + before + [("values", b, 0)]
        order += [("mix", b - 1, 1)] if b else []
        order += [("scores", b, 0), ("project", b, 1), ("mix", b, 0), ("values", b, 1)]
    return order + [("scores", LAST, 1), ("mix", LAST, 1)]


ORDER = schedule()


def units_of(phase, b):
    k = KIND[b]
    if phase == "prelude":
        return []
    if phase == "project":
        u = ["T"]
        if k == "rope":
            u += (["CT"] if CROSS[b] else []) + ["Q0", "Q1", "K0", "K1"]
        if k == "flat":
            u += ["Q0", "Q1", "K0", "K1"]
        if k == "small" and CROSS[b]:
            u += ["C"]
        if b == L3_SELF:
            u += ["G"]
        return u
    if phase == "values":
        if k in ("rope", "flat"):
            return ["VW0", "VW1", "VW2", "VW3"]
        if k == "ff":
            return ["U0", "U1"] if b >= L2_FF else ["U0"]
        return ["HC", "V"] if b == L3_SELF else ["QKV"]
    if phase == "scores":
        u = ["QT0", "KT0", "QT1", "KT1"] if k == "rope" else []
        if b == L3_SELF:
            u = ["VAR"]
        return u + ([f"S{g}" for g in range(4)] if k != "ff" else [])
    if k == "ff":
        return ["D"]
    return [f"PT{g}" for g in range(4)] + ["PV"] + (["PJ"] if k == "small" else [])


UNIT, _u = {}, 0
for _phase, _b, _par in ORDER:
    for _n in units_of(_phase, _b):
        UNIT[_b, _par, _n] = (_u % BANKS, _u // BANKS)
        _u += 1
PER_TURN = [(_u - b + BANKS - 1) // BANKS for b in range(BANKS)]
SETUP_UNITS = 17
SETUP = [(SETUP_UNITS - b + BANKS - 1) // BANKS for b in range(BANKS)]


def counts_of(phase, b):
    c = {}
    k = KIND[b]
    if phase == "prelude":
        c["ln"] = 2
    if phase == "mix" and b < LAST:
        c["ln"] = 1
    if phase == "project" and k == "rope":
        c["rope"] = 4
    if phase == "scores" and k != "ff":
        c["soft"] = 4
    if phase == "scores" and b == L3_SELF:
        c["head"] = 1
    if phase == "values" and k == "small":
        c["vmask"] = 1
    if phase == "values" and b == L3_FF:
        c["act"] = 1
    return c


FIRST, TOTAL = {}, {}
for _phase, _b, _par in ORDER:
    for _n, _k in counts_of(_phase, _b).items():
        FIRST[_n, _phase, _b, _par] = TOTAL.get(_n, 0)
        TOTAL[_n] = TOTAL.get(_n, 0) + _k

DVE_STEPS = 86

WEIGHTS = ["wq0", "wk0", "cq0", "ck0", "f10", "f20",
           "qkv1", "proj1", "ctx1", "cqkv1", "out1", "f11", "f21",
           "wq2", "wk2", "cq2", "ck2", "f12", "f22",
           "gate3", "cond3", "cqkv3", "out3", "f13", "f23"]
LAYER_OF = {n: int(n[-1]) for n in WEIGHTS}
LAYER_COUNT = [sum(l == i for l in LAYER_OF.values()) for i in range(4)]


def tile_of(g, j):
    return DH * (g % 2), T4 * (g // 2) + j


def build(nc, x, ctx, ctx_t, cond_t, vecs, lnc, rows, consts, setup_w, w, out):
    fp32 = mybir.dt.float32
    ALU = mybir.AluOpType
    ACT = mybir.ActivationFunctionType
    AX = mybir.AxisListType.X
    stack = ExitStack()
    with stack:
        def sb(name, *shape):
            return stack.enter_context(nc.sbuf_tensor(name, list(shape), fp32))

        def sem(name):
            return stack.enter_context(nc.semaphore(name))

        W = {n: sb("w_" + n, *a.shape) for n, a in w.items()}
        M = {n: sb("m_" + n, r, H * D) for n, r in (("sa0", D), ("ca0", CD), ("sa2", D), ("ca2", CD))}
        C = sb("consts", 128, NCONST)
        V = sb("vecs", 128, len(VEC))
        LNC = sb("lnc", CD, 2)
        R = sb("rows", 128, len(ROW) * D)
        mod = sb("mod", 128, S, 2 * NMOD)
        condT = sb("condT", 128, S)
        siluT = sb("siluT", 128, S)
        silu_t = sb("silu_t", 128, 2 * S)
        raw = sb("raw", 128, 2 * NMOD, S)
        qn_scaled = sb("qn_scaled", 128, 2)
        prod = sb("prod", 128, 2, 2, BANK)

        def pair(name, *shape):
            return [sb(f"{name}{p}", *shape) for p in range(2)]

        xin = pair("xin", N, D)
        cin = pair("cin", N, CD)
        ctxT = pair("ctxT", CD, N)
        X = pair("X", N, D)
        xb = pair("xb", N, D)
        gb = pair("gb", N, D)
        xn = pair("xn", N, D)
        cn = pair("cn", N, CD)
        hT = pair("hT", D, N)
        kvT = pair("kvT", D, N)
        modc = pair("modc", 128, 2 * NMOD)
        cb = pair("cb", 128, N)
        gates = pair("gates", N, 3 * D)
        st = pair("st", 128, 2, 6)
        mv = pair("mv", 128, 2, 2)
        ve = pair("ve", 128, 2)
        rstd = pair("rstd", 128, 2)
        negmax = pair("negmax", N, H)
        sums = pair("sums", N, H)
        rinv = pair("rinv", N, H)
        outT = pair("outT", D, N)
        qT = pair("qT", 128, H // 2, N)
        kT = pair("kT", 128, H // 2, N)
        VW = pair("VW", N, H * D)
        E = pair("E", N, H, N)
        PT = pair("PT", N, H * N)
        rot = [PT[p][:, :].rearrange("p (s c) -> p s c", s=2) for p in range(2)]
        vb = [PT[p][:, 0:D] for p in range(2)]
        vmask = [VW[p][:, 0:T4 * D].rearrange("p (j f) -> p j f", j=T4) for p in range(2)]
        hc = [VW[p][:, 1024:1024 + N] for p in range(2)]
        hsq = [VW[p][:, 1152:1152 + N] for p in range(2)]
        hve = [VW[p][:, 1280:1280 + N] for p in range(2)]
        hrs = [VW[p][:, 1408:1408 + N] for p in range(2)]
        hz = [VW[p][:, 1536:1536 + N] for p in range(2)]
        hk = [VW[p][:, 1664:1664 + N] for p in range(2)]
        res = [VW[p][:, 1792:1792 + D] for p in range(2)]
        hid = [E[p][:, 0:T4, :] for p in range(2)]
        act_out = [E[p][:, T4:2 * T4, :] for p in range(2)]
        mid = [E[p][:, 2 * T4:3 * T4, :] for p in range(2)]

        stage = {}
        for n, src in setup_w.items():
            stage[n] = {"vt_sa0": E[0][:, 0:8, :], "wo_sa0": E[0][:, 8:16, :],
                        "vt_sa2": PT[0][:, 0:1024].rearrange("p (t i) -> p t i", t=8),
                        "wo_sa2": PT[0][:, 1024:2048].rearrange("p (t i) -> p t i", t=8),
                        "vt_ca0": VW[0][:, 0:768].rearrange("p (t i) -> p t i", t=8),
                        "wo_ca0": VW[0][:, 1024:2048].rearrange("p (t i) -> p t i", t=8),
                        "vt_ca2": E[1][:, 0:6, :].rearrange("p a b -> p (a b)").rearrange("p (t i) -> p t i", t=8),
                        "wo_ca2": E[1][:, 8:16, :],
                        "mod_lin": PT[1][:, 0:10 * D],
                        "mod_silu": VW[1][:, 0:12 * D]}[n]

        ps = stack.enter_context(nc.psum_tensor("ps", [128, BANKS, BANK], fp32))

        bank_full = [sem(f"bank_full{b}") for b in range(BANKS)]
        bank_drained = [sem(f"bank_drained{b}") for b in range(BANKS)]
        small_loaded = sem("small_loaded")
        setup_loaded = {n: sem("setup_loaded_" + n) for n in ("sa0", "ca0", "sa2", "ca2", "mod")}
        layer_loaded = [sem(f"layer_loaded{i}") for i in range(4)]
        x_loaded = [sem(f"x_loaded{p}") for p in range(2)]
        ctxT_loaded = [sem(f"ctxT_loaded{p}") for p in range(2)]
        silu_in = sem("silu_in")
        silu_ready = sem("silu_ready")
        setup_step = sem("setup_step")
        var_ready = sem("var_ready")
        rstd_ready = sem("rstd_ready")
        norm_ready = sem("norm_ready")
        rotated_ready = sem("rotated_ready")
        negmax_ready = sem("negmax_ready")
        rinv_ready = sem("rinv_ready")
        probs_ready = sem("probs_ready")
        hsq_ready = sem("hsq_ready")
        hrstd_ready = sem("hrstd_ready")
        heads_ready = sem("heads_ready")
        vmask_ready = sem("vmask_ready")
        act_ready = sem("act_ready")
        dve_step = sem("dve_step")
        out_ready = sem("out_ready")
        out_done = [sem(f"out_done{p}") for p in range(2)]

        def bank(u, a=0, b=BANK):
            return ps[:, u[0], a:b]

        def c(name):
            return C[:, CONST[name]]

        def v(name):
            return V[:, VEC[name]:VEC[name] + 1]

        def row(name, n=1):
            return R[:, ROW[name] * D:(ROW[name] + n) * D]

        known = {}

        def wait_turn(eng, it, semaphore, per_turn, count):
            if known.get((eng, semaphore.name), 0) < count:
                known[eng, semaphore.name] = count
                eng.wait_ge(semaphore, it * per_turn + count)

        def claim(eng, it, u):
            wait_turn(eng, it, bank_drained[u[0]], PER_TURN[u[0]], SETUP[u[0]] + u[1])

        def filled(eng, it, u):
            wait_turn(eng, it, bank_full[u[0]], PER_TURN[u[0]], SETUP[u[0]] + u[1] + 1)

        def drained(eng, it, u):
            wait_turn(eng, it, bank_drained[u[0]], PER_TURN[u[0]], SETUP[u[0]] + u[1] + 1)

        def given(eng, it, semaphore, kind, phase, b, par, k=0):
            wait_turn(eng, it, semaphore, TOTAL[kind], FIRST[kind, phase, b, par] + k + 1)

        def given_ln(eng, it, semaphore, b, par):
            given(eng, it, semaphore, "ln", *(("mix", b - 1, par) if b else ("prelude", 0, par)))

        block = stack.enter_context(nc.Block())

        @block.sync
        def _(sp):
            def at(dram, i):
                return dram[bass.ds(i, 1)].rearrange("a n d -> (a n) d")

            sp.dma_start(condT[:, :], cond_t).then_inc(small_loaded, 16)
            sp.dma_start(V[:, :], vecs).then_inc(small_loaded, 16)
            sp.dma_start(stage["mod_lin"], setup_w["mod_lin"]).then_inc(setup_loaded["mod"], 16)
            sp.dma_start(stage["mod_silu"], setup_w["mod_silu"]).then_inc(setup_loaded["mod"], 16)
            for n in ("sa0", "ca0", "sa2", "ca2"):
                for k in ("vt_", "wo_"):
                    sp.dma_start(stage[k + n], setup_w[k + n].rearrange("(t p) i -> p t i", t=8))\
                      .then_inc(setup_loaded[n], 16)
                if n == "sa0":
                    sp.dma_start(C[:, :], consts).then_inc(small_loaded, 16)
                    sp.dma_start(LNC[:, :], lnc).then_inc(small_loaded, 16)
                    sp.dma_start(R[:, :], rows.partition_broadcast(128)).then_inc(small_loaded, 16)
                    for p in range(2):
                        sp.dma_start(xin[p][:, :], x[p]).then_inc(x_loaded[p], 16)
                        sp.dma_start(cin[p][:, :], ctx[p]).then_inc(x_loaded[p], 16)
            for n in W:
                sp.dma_start(W[n][:], w[n]).then_inc(layer_loaded[LAYER_OF[n]], 16)
            for p in range(2):
                sp.dma_start(ctxT[p][:, :], ctx_t[p]).then_inc(ctxT_loaded[p], 16)
            with sp.Fori(0, PAIRS - 1) as it:
                read = [sp.snap(it * TOTAL["ln"] + (FIRST["ln", "prelude", 0, p] + 2)) for p in range(2)]
                stored = sp.snap(it * 16 + 16)
                produced = [sp.snap(it * 2 + (p + 1)) for p in range(2)]
                this = [it * 2 + p for p in range(2)]
                following = [it * 2 + (2 + p) for p in range(2)]
                for p in range(2):
                    sp.wait_ge(norm_ready, read[p])
                    sp.dma_start(xin[p][:, :], at(x, following[p])).then_inc(x_loaded[p], 16)
                    sp.dma_start(cin[p][:, :], at(ctx, following[p])).then_inc(x_loaded[p], 16)
                for p in range(2):
                    sp.wait_ge(out_ready, produced[p])
                    sp.dma_start(at(out, this[p]), X[p][:, :]).then_inc(out_done[p], 16)
                for p in range(2):
                    sp.wait_ge(out_done[p], stored)
                    sp.dma_start(ctxT[p][:, :], at(ctx_t, following[p])).then_inc(ctxT_loaded[p], 16)
            for p in range(2):
                sp.wait_ge(out_ready, 2 * (PAIRS - 1) + p + 1)
                sp.dma_start(out[S - 2 + p], X[p][:, :]).then_inc(out_done[p], 16)
            for p in range(2):
                sp.wait_ge(out_done[p], 16 * PAIRS)

        @block.tensor
        def _(pe):
            mm = nc.tensor.matmul

            def set_up():
                pe.wait_ge(small_loaded, 16 * 5)
                pe.wait_ge(setup_loaded["mod"], 32)
                pe.wait_ge(silu_ready, 1)
                lin = silu = 0
                for i in range(22):
                    if i < 4 or 10 <= i < 16:
                        lhs, rhs, lin = stage["mod_lin"][:, lin * D:(lin + 1) * D], condT, lin + 1
                    else:
                        lhs, rhs, silu = stage["mod_silu"][:, silu * D:(silu + 1) * D], siluT, silu + 1
                    last = mm(ps[:, 0, i * S:(i + 1) * S], lhs, rhs[:, :], start=True, stop=True)
                last.then_inc(bank_full[0], 1)
                u = 1
                for n in ("sa0", "ca0", "sa2", "ca2"):
                    pe.wait_ge(setup_loaded[n], 32)
                    rows_ = M[n].shape[0]
                    for g in (0, 2):
                        for i in range(2):
                            if u + i >= BANKS:
                                pe.wait_ge(bank_drained[(u + i) % BANKS], (u + i) // BANKS)
                        for j in range(T4):
                            for i in range(2):
                                p0, t = tile_of(g + i, j)
                                last = mm(ps[0:rows_, (u + i) % BANKS, j * D:(j + 1) * D],
                                          stage["vt_" + n][p0:p0 + DH, t, :], stage["wo_" + n][p0:p0 + DH, t, :],
                                          start=True, stop=True)
                                if j == T4 - 1:
                                    last.then_inc(bank_full[(u + i) % BANKS], 1)
                        u += 2

            def project(it, b, par):
                k = KIND[b]
                full = lambda last, u: last.then_inc(bank_full[u[0]], 1)
                u = UNIT[b, par, "T"]
                given_ln(pe, it, norm_ready, b, par)
                claim(pe, it, u)
                full(nc.tensor.transpose(bank(u, 0, N), xn[par][:, :], c("ident")), u)
                if b % 3 == 0:
                    pe.wait_ge(layer_loaded[b // 3], 16 * LAYER_COUNT[b // 3])
                if k == "rope" and CROSS[b]:
                    u = UNIT[b, par, "CT"]
                    claim(pe, it, u)
                    full(nc.tensor.transpose(ps[0:CD, u[0], 0:N], cn[par][:, :], c("ident")), u)
                if k == "small" and CROSS[b]:
                    u = UNIT[b, par, "C"]
                    claim(pe, it, u)
                    pe.wait_ge(ctxT_loaded[par], it * 16 + 16)
                    full(mm(bank(u, 0, N), W["ctx1" if b == 4 else "cond3"][:, :], ctxT[par][:, :],
                            start=True, stop=True), u)
                if b == L3_SELF:
                    u = UNIT[b, par, "G"]
                    claim(pe, it, u)
                    full(mm(bank(u, 0, 3 * D), cb[par][:, :], W["gate3"][:, :], start=True, stop=True), u)
                if k == "rope":
                    wide = "c" if CROSS[b] else "w"
                    drained(pe, it, UNIT[b, par, "T"])
                    for n, src, wt in (("Q", hT[par][:, :], W[wide + "q0"]),
                                       ("K", kvT[par][0:CD, :] if CROSS[b] else hT[par][:, :], W[wide + "k0"])):
                        if n == "K" and CROSS[b]:
                            drained(pe, it, UNIT[b, par, "CT"])
                        for i in range(2):
                            u = UNIT[b, par, f"{n}{i}"]
                            claim(pe, it, u)
                            full(mm(bank(u), src, wt[:, i * BANK:(i + 1) * BANK], start=True, stop=True), u)
                if k == "flat":
                    wide = "c" if CROSS[b] else "w"
                    drained(pe, it, UNIT[b, par, "T"])
                    for n, src, wt in (("Q", hT[par][:, :], W[wide + "q2"]),
                                       ("K", ctxT[par][:, :] if CROSS[b] else hT[par][:, :], W[wide + "k2"])):
                        for i in range(2):
                            u = UNIT[b, par, f"{n}{i}"]
                            claim(pe, it, u)
                            for j in range(T4):
                                t = T4 * i + j
                                last = mm(bank(u, j * N, (j + 1) * N), wt[:, t * 128:(t + 1) * 128], src,
                                          start=True, stop=True)
                            full(last, u)

            def values(it, b, par):
                k = KIND[b]
                full = lambda last, u: last.then_inc(bank_full[u[0]], 1)
                if k in ("rope", "flat"):
                    if not CROSS[b]:
                        src, m = hT[par][:, :], M["sa0" if b == 0 else "sa2"]
                    elif k == "rope":
                        src, m = kvT[par][0:CD, :], M["ca0"]
                    else:
                        src, m = ctxT[par][:, :], M["ca2"]
                    for i in range(4):
                        u = UNIT[b, par, f"VW{i}"]
                        claim(pe, it, u)
                        full(mm(bank(u), src, m[:, i * BANK:(i + 1) * BANK], start=True, stop=True), u)
                elif k == "ff":
                    drained(pe, it, UNIT[b, par, "T"])
                    w1 = W[f"f1{b // 3}"]
                    for i in range(len(units_of("values", b))):
                        u = UNIT[b, par, f"U{i}"]
                        claim(pe, it, u)
                        for j in range(T4):
                            t = T4 * i + j
                            last = mm(bank(u, j * N, (j + 1) * N), w1[:, t * 128:(t + 1) * 128], hT[par][:, :],
                                      start=True, stop=True)
                        full(last, u)
                elif b == L3_SELF:
                    drained(pe, it, UNIT[b, par, "T"])
                    u = UNIT[b, par, "HC"]
                    claim(pe, it, u)
                    full(mm(bank(u, 0, N), c("center"), hT[par][:, :], start=True, stop=True), u)
                    u = UNIT[b, par, "V"]
                    claim(pe, it, u)
                    full(nc.tensor.transpose(bank(u, 0, D), hT[par][:, :], c("ident")), u)
                else:
                    drained(pe, it, UNIT[b, par, "T"])
                    u = UNIT[b, par, "QKV"]
                    wt = W[{3: "qkv1", 4: "cqkv1", 10: "cqkv3"}[b]]
                    src = hT[par]
                    if CROSS[b]:
                        drained(pe, it, UNIT[b, par, "C"])
                        src = kvT[par]
                    claim(pe, it, u)
                    mm(bank(u, 0, N), wt[:, 0:D], hT[par][:, :], start=True, stop=True)
                    mm(bank(u, N, 2 * N), wt[:, D:2 * D], src[:, :], start=True, stop=True)
                    full(mm(bank(u, 2 * N, 3 * N), src[:, :], wt[:, 2 * D:3 * D], start=True, stop=True), u)

            def scores(it, b, par):
                k = KIND[b]
                if k == "ff":
                    return
                full = lambda last, u: last.then_inc(bank_full[u[0]], 1)
                if k == "rope":
                    for i, n in enumerate(["QT0", "KT0", "QT1", "KT1"]):
                        u = UNIT[b, par, n]
                        which, half = i % 2, i // 2
                        given(pe, it, rotated_ready, "rope", "project", b, par, 2 * which + half)
                        claim(pe, it, u)
                        for j in range(T4):
                            a = half * BANK + j * 128
                            last = nc.tensor.transpose(bank(u, j * N, (j + 1) * N),
                                                       rot[par][:, which, a:a + 128], c("ident"))
                        full(last, u)
                if b == L3_SELF:
                    u = UNIT[b, par, "VAR"]
                    claim(pe, it, u)
                    given(pe, it, hsq_ready, "head", "scores", b, par)
                    full(mm(bank(u, 0, N), c("mean8"), hsq[par], start=True, stop=True), u)
                    given(pe, it, heads_ready, "head", "scores", b, par)
                elif k == "small":
                    drained(pe, it, UNIT[b, par, "QKV"])
                if k == "small":
                    for g in range(4):
                        u = UNIT[b, par, f"S{g}"]
                        p0 = 32 * g
                        claim(pe, it, u)
                        full(mm(bank(u), qT[par][p0:p0 + 32, 0, :], kT[par][p0:p0 + 32, 0:T4, :],
                                start=True, stop=True, tile_position=(p0, 0)), u)
                    return
                for half in range(2):
                    pair_ = [UNIT[b, par, f"S{2 * half + i}"] for i in range(2)]
                    for n in ((f"QT{half}", f"KT{half}") if k == "rope" else (f"Q{half}", f"K{half}")):
                        drained(pe, it, UNIT[b, par, n])
                    for u in pair_:
                        claim(pe, it, u)
                    for j in range(T4):
                        for i, u in enumerate(pair_):
                            p0, t = tile_of(2 * half + i, j)
                            last = mm(bank(u, j * N, (j + 1) * N), qT[par][p0:p0 + DH, t, :],
                                      kT[par][p0:p0 + DH, t, :], start=True, stop=True)
                            if j == T4 - 1:
                                full(last, u)

            def mix(it, b, par):
                k = KIND[b]
                full = lambda last, u: last.then_inc(bank_full[u[0]], 1)
                if k == "ff":
                    u = UNIT[b, par, "D"]
                    drained(pe, it, UNIT[b, par, "U1" if b == L3_FF else "U0"])
                    claim(pe, it, u)
                    w2 = W[f"f2{b // 3}"]
                    for t in range(T4):
                        last = mm(bank(u, 0, D), hid[par][:, t, :], w2[:, t, :], start=(t == 0), stop=(t == T4 - 1))
                    full(last, u)
                    return
                for g in range(4):
                    u = UNIT[b, par, f"PT{g}"]
                    claim(pe, it, u)
                    given(pe, it, probs_ready, "soft", "scores", b, par, g)
                    for j in range(T4):
                        last = nc.tensor.transpose(bank(u, j * N, (j + 1) * N), E[par][:, T4 * g + j, :], c("ident"))
                    full(last, u)
                u = UNIT[b, par, "PV"]
                if k == "small":
                    given(pe, it, vmask_ready, "vmask", "values", b, par)
                else:
                    drained(pe, it, UNIT[b, par, "VW3"])
                claim(pe, it, u)
                for g in range(4):
                    drained(pe, it, UNIT[b, par, f"PT{g}"])
                    for j in range(T4):
                        h = T4 * g + j
                        pt = PT[par][:, h * N:(h + 1) * N]
                        if k == "small":
                            p0 = 32 * g
                            last = mm(ps[p0:p0 + 32, u[0], 0:N], vmask[par][:, j, p0:p0 + 32], pt,
                                      start=(j == 0), stop=(j == T4 - 1), tile_position=(0, p0))
                        else:
                            last = mm(bank(u, 0, D), pt, VW[par][:, h * D:(h + 1) * D],
                                      start=(h == 0), stop=(h == H - 1))
                full(last, u)
                if k == "small":
                    drained(pe, it, u)
                    u = UNIT[b, par, "PJ"]
                    claim(pe, it, u)
                    wp = {3: W.get("proj1"), 4: W.get("out1"), 10: W.get("out3")}.get(b)
                    full(mm(bank(u, 0, D), outT[par][:, :], wp[:, :] if wp is not None else c("ident"),
                            start=True, stop=True), u)

            set_up()
            with pe.Fori(0, PAIRS) as it:
                for phase, b, par in ORDER:
                    if phase != "prelude":
                        {"project": project, "values": values, "scores": scores, "mix": mix}[phase](it, b, par)

        @block.scalar
        def _(act):
            drain = lambda last, u: last.then_inc(bank_drained[u[0]], 1)

            def set_up():
                act.wait_ge(small_loaded, 16 * 5)
                nc.scalar.activation(silu_t[:, 0:S], condT[:, :], ACT.Tanh, scale=0.5).then_inc(silu_in, 1)
                u = 1
                for n in ("sa0", "ca0", "sa2", "ca2"):
                    r = M[n].shape[0]
                    for g in range(4):
                        act.wait_ge(bank_full[u % BANKS], u // BANKS + 1)
                        nc.scalar.activation(M[n][:, g * BANK:(g + 1) * BANK], ps[0:r, u % BANKS, :], ACT.Copy)\
                          .then_inc(bank_drained[u % BANKS], 1)
                        u += 1

            def project(it, b, par):
                u = UNIT[b, par, "T"]
                filled(act, it, u)
                m = 2 * MODPAIR[b]
                drain(nc.scalar.activation(hT[par][:, :], bank(u, 0, N), ACT.Identity,
                                           scale=modc[par][:, m:m + 1], bias=modc[par][:, m + 1:m + 2]), u)
                if KIND[b] == "rope" and CROSS[b]:
                    u = UNIT[b, par, "CT"]
                    filled(act, it, u)
                    drain(nc.scalar.activation(kvT[par][0:CD, :], ps[0:CD, u[0], 0:N], ACT.Identity,
                                               scale=LNC[:, 0:1], bias=LNC[:, 1:2]), u)

            def values(it, b, par):
                k = KIND[b]
                if k in ("rope", "flat"):
                    for i in range(4):
                        u = UNIT[b, par, f"VW{i}"]
                        filled(act, it, u)
                        drain(nc.scalar.activation(VW[par][:, i * BANK:(i + 1) * BANK], bank(u), ACT.Copy), u)
                if k == "ff" and b < L2_FF:
                    u = UNIT[b, par, "U0"]
                    filled(act, it, u)
                    f, name = (ACT.Gelu, "ff1_0_") if b == 2 else (ACT.Gelu_apprx_tanh, "fc1_")
                    for t in range(T4):
                        last = nc.scalar.activation(hid[par][:, t, :], bank(u, t * N, (t + 1) * N), f,
                                                    bias=v(f"{name}{t}"))
                    drain(last, u)
                if b == L2_FF:
                    u = UNIT[b, par, "U1"]
                    filled(act, it, u)
                    for t in range(T4):
                        last = nc.scalar.activation(act_out[par][:, t, :], bank(u, t * N, (t + 1) * N), ACT.Gelu,
                                                    bias=v(f"ff1_2_{T4 + t}"))
                    drain(last, u)
                if b == L3_FF:
                    u = UNIT[b, par, "U0"]
                    filled(act, it, u)
                    nc.scalar.activation(act_out[par], bank(u).rearrange("p (t n) -> p t n", t=T4), ACT.Tanh,
                                         scale=0.5).then_inc(act_ready, 1)

            def scores(it, b, par):
                k = KIND[b]
                if k == "ff":
                    return
                if k == "rope":
                    for n in ("QT0", "KT0", "QT1", "KT1"):
                        u = UNIT[b, par, n]
                        half = int(n[2])
                        filled(act, it, u)
                        dst = (qT if n[0] == "Q" else kT)[par]
                        drain(nc.scalar.activation(dst[:, T4 * half:T4 * half + T4, :],
                                                   bank(u).rearrange("p (t n) -> p t n", t=T4), ACT.Copy), u)
                for g in range(4):
                    u = UNIT[b, par, f"S{g}"]
                    given(act, it, negmax_ready, "soft", "scores", b, par, g)
                    for j in range(T4):
                        h = T4 * g + j
                        last = nc.scalar.activation(E[par][:, h, :], bank(u, j * N, (j + 1) * N), ACT.Exp,
                                                    bias=negmax[par][:, h:h + 1],
                                                    accum_out=sums[par][:, h:h + 1])
                    drain(last, u)

            def mix(it, b, par):
                if KIND[b] == "small":
                    u = UNIT[b, par, "PV"]
                    filled(act, it, u)
                    drain(nc.scalar.activation(outT[par][:, :], bank(u, 0, N), ACT.Copy), u)

            set_up()
            with act.Fori(0, PAIRS) as it:
                for phase, b, par in ORDER:
                    if phase != "prelude":
                        {"project": project, "values": values, "scores": scores, "mix": mix}[phase](it, b, par)

        @block.gpsimd
        def _(pool):
            tt = nc.gpsimd.tensor_tensor

            def norm_power(it, phase, b, par, k=0):
                given(pool, it, var_ready, "ln", phase, b, par, k)
                tt(rstd[par][:, k:k + 1], ve[par][:, k:k + 1], c("neghalf"), ALU.pow).then_inc(rstd_ready, 1)

            pool.wait_ge(small_loaded, 16 * 5)
            with pool.Fori(0, PAIRS) as it:
                for phase, b, par in ORDER:
                    if phase == "prelude":
                        norm_power(it, "prelude", 0, par, 0)
                        norm_power(it, "prelude", 0, par, 1)
                    if phase == "project" and KIND[b] == "rope":
                        for i in range(4):
                            n = FIRST["rope", "project", b, par] + i
                            drained(pool, it, UNIT[b, par, ["Q0", "Q1", "K0", "K1"][i]])
                            tt(rot[par][:, i // 2, (i % 2) * BANK:(i % 2 + 1) * BANK],
                               prod[:, n % 2, 0, :], prod[:, n % 2, 1, :], ALU.add).then_inc(rotated_ready, 1)
                    if phase == "scores" and b == L3_SELF:
                        drained(pool, it, UNIT[b, par, "VAR"])
                        tt(hrs[par], hve[par], c("neghalf").broadcast_to([128, N]), ALU.pow).then_inc(hrstd_ready, 1)
                    if phase == "scores" and KIND[b] != "ff":
                        for g in range(4):
                            given(pool, it, rinv_ready, "soft", "scores", b, par, g)
                            e = E[par][:, T4 * g:T4 * g + T4, :]
                            tt(e, e, rinv[par][:, T4 * g:T4 * g + T4].unsqueeze(2).broadcast_to([N, T4, N]),
                               ALU.mult).then_inc(probs_ready, 1)
                    if phase == "mix" and b < LAST:
                        norm_power(it, "mix", b, par)

        @block.vector
        def _(dve):
            tt, ts = nc.vector.tensor_tensor, nc.vector.tensor_scalar
            drain = lambda last, u: last.then_inc(bank_drained[u[0]], 1)
            steps = [0]
            turn = [None]
            residual = [None, None]

            def step(ins):
                ins.then_inc(dve_step, 1)
                steps[0] += 1
                return steps[0]

            def after(n):
                dve.wait_ge(dve_step, turn[0] * DVE_STEPS + n)

            def set_up():
                n = [0]

                def link(ins):
                    ins.then_inc(setup_step, 1)
                    n[0] += 1
                    dve.wait_ge(setup_step, n[0])

                dve.wait_ge(small_loaded, 16 * 5)
                dve.wait_ge(silu_in, 1)
                link(nc.vector.scalar_tensor_tensor(out=silu_t[:, S:2 * S], in0=silu_t[:, 0:S], scalar=1.0,
                                                    in1=condT[:, :], op0=ALU.add, op1=ALU.mult))
                ts(siluT[:, :], silu_t[:, S:2 * S], 0.5, None, ALU.mult).then_inc(silu_ready, 1)
                link(ts(qn_scaled[:, :], V[:, VEC["qn_w"]:VEC["qn_w"] + 2], float(HD) ** -0.5, None, ALU.mult))
                dve.wait_ge(bank_full[0], 1)
                last = tt(raw[:, :, :], ps[:, 0, 0:22 * S].rearrange("p (i s) -> p i s", s=S),
                          V[:, VEC["raw0"]:VEC["raw0"] + 22].unsqueeze(2).broadcast_to([128, 22, S]), ALU.add)
                last.then_inc(bank_drained[0], 1)
                dve.wait_ge(bank_drained[0], 1)
                for i in range(2):
                    g, s = raw[:, 2 * i, :], raw[:, 2 * i + 1, :]
                    lw, lb = v(f"ln{i + 1}_w"), v(f"ln{i + 1}_b")
                    link(ts(g, g, 1.0, None, ALU.add))
                    ts(mod[:, :, 2 * i], g, lw, None, ALU.mult)
                    link(ts(g, g, lb, None, ALU.mult))
                    link(tt(mod[:, :, 2 * i + 1], g, s, ALU.add))
                for j in range(2, NMOD):
                    scale, shift = (2 * j, 2 * j + 1) if 5 <= j < 8 else (2 * j + 1, 2 * j)
                    ts(mod[:, :, 2 * j], raw[:, scale, :], 1.0, None, ALU.add)
                    last = nc.vector.tensor_copy(mod[:, :, 2 * j + 1], raw[:, shift, :])
                link(last)

            def norm(it, par, b):
                phase = ("mix", b - 1) if b else ("prelude", 0)
                xt = X[par] if b else xin[par]
                todo = [(xt, xn[par], 0, EPS[b])] + ([(cin[par], cn[par], 1, EPS_CTX)] if b == 0 else [])
                for src, _, i, _ in todo:
                    n = step(nc.vector.bn_stats(st[par][:, i, :], src[:, :]))
                after(n)
                if b == L3_CROSS:
                    n = step(tt(gb[par][:, :], gates[par][:, D:2 * D], row(OUT_ROW[b]), ALU.mult))
                elif OUT_ROW[b] is None:
                    n = step(nc.vector.tensor_copy(xb[par][:, :], xt[:, :]))
                else:
                    n = step(tt(xb[par][:, :], xt[:, :], row(OUT_ROW[b]), ALU.add))
                for _, _, i, _ in todo:
                    m = step(nc.vector.bn_aggr(mv[par][:, i, :], st[par][:, i, :]))
                if b == L3_CROSS:
                    after(n)
                    n = step(tt(xb[par][:, :], xt[:, :], gb[par][:, :], ALU.add))
                residual[par] = n
                after(m)
                for _, _, i, eps in todo:
                    ts(ve[par][:, i:i + 1], mv[par][:, i, 1:2], eps, None, ALU.add).then_inc(var_ready, 1)
                for src, dst, i, _ in todo:
                    given(dve, it, rstd_ready, "ln", *phase, par, i)
                    ts(dst[:, :], src[:, :], mv[par][:, i, 0:1], rstd[par][:, i:i + 1], ALU.subtract, ALU.mult)\
                        .then_inc(norm_ready, 1)

            def prelude(it, b, par):
                dve.wait_ge(x_loaded[par], it * 32 + 32)
                nc.vector.tensor_copy(modc[par][:, :], mod[:, bass.ds(it * 2 + par, 1), :].rearrange("p a m -> p (a m)"))
                nc.vector.tensor_copy(cb[par][:, :], siluT[:, bass.ds(it * 2 + par, 1)].broadcast_to([128, N]))
                norm(it, par, 0)

            def project(it, b, par):
                k = KIND[b]
                if k == "rope":
                    for i, n in enumerate(["Q0", "Q1", "K0", "K1"]):
                        u = UNIT[b, par, n]
                        m = FIRST["rope", "project", b, par] + i
                        if m >= 2:
                            dve.wait_ge(rotated_ready, it * TOTAL["rope"] + (m - 1))
                        filled(dve, it, u)
                        q = bank(u).rearrange("p (h i e) -> p h i e", h=8, e=2)
                        cos, sin = c("cosq" if i < 2 else "cosk"), c("sinq" if i < 2 else "sink")
                        a = prod[:, m % 2, 0, :].rearrange("p (h i) -> p h i", h=8)
                        s = prod[:, m % 2, 1, :].rearrange("p (h i e) -> p h i e", h=8, e=2)
                        sn = sin.rearrange("p (i e) -> p i e", e=2)
                        tt(a, bank(u).rearrange("p (h i) -> p h i", h=8),
                           cos.unsqueeze(1).broadcast_to([128, 8, DH]), ALU.mult)
                        tt(s[:, :, :, 0], q[:, :, :, 1], sn[:, :, 0].unsqueeze(1).broadcast_to([128, 8, 32]), ALU.mult)
                        drain(tt(s[:, :, :, 1], q[:, :, :, 0],
                                 sn[:, :, 1].unsqueeze(1).broadcast_to([128, 8, 32]), ALU.mult), u)
                if k == "flat":
                    for n in ("Q0", "Q1", "K0", "K1"):
                        u = UNIT[b, par, n]
                        i = int(n[1])
                        filled(dve, it, u)
                        src = bank(u).rearrange("p (t n) -> p t n", t=T4)
                        if n[0] == "Q":
                            drain(ts(qT[par][:, T4 * i:T4 * i + T4, :], src, float(DH) ** -0.5, None, ALU.mult), u)
                        else:
                            drain(nc.vector.tensor_copy(kT[par][:, T4 * i:T4 * i + T4, :], src), u)
                if k == "small" and CROSS[b]:
                    u = UNIT[b, par, "C"]
                    filled(dve, it, u)
                    drain(ts(kvT[par][:, :], bank(u, 0, N), v("bctx" if b == 4 else "bcond"), None, ALU.add), u)
                if b == L3_SELF:
                    u = UNIT[b, par, "G"]
                    filled(dve, it, u)
                    drain(tt(gates[par][:, :], bank(u, 0, 3 * D), row("g0", 3), ALU.add), u)

            def values(it, b, par):
                k = KIND[b]
                masks = c("rowmask")
                cm = c("colmask").rearrange("p (j f) -> p j f", j=T4)
                if k == "small" and b != L3_SELF:
                    u = UNIT[b, par, "QKV"]
                    filled(dve, it, u)
                    bq, bk, bv = {3: (v("bq1"), v("bk1"), row("bv1")), 4: (0.0, 0.0, None),
                                  10: (v("bq3"), v("bk3"), row("bv3"))}[b]
                    ts(qT[par][:, 0, :], bank(u, 0, N), bq, float(HD) ** -0.5, ALU.add, ALU.mult)
                    for j in range(T4):
                        ts(kT[par][:, j, :], bank(u, N, 2 * N), bk, masks[:, j:j + 1], ALU.add, ALU.mult)
                    if bv is None:
                        drain(nc.vector.tensor_copy(vb[par], bank(u, 2 * N, 3 * N)), u)
                    else:
                        drain(tt(vb[par], bank(u, 2 * N, 3 * N), bv, ALU.add), u)
                    drained(dve, it, u)
                    tt(vmask[par], vb[par].unsqueeze(1).broadcast_to([N, T4, D]), cm, ALU.mult)\
                        .then_inc(vmask_ready, 1)
                if b == L3_SELF:
                    u = UNIT[b, par, "HC"]
                    filled(dve, it, u)
                    drain(nc.vector.tensor_copy(hc[par], bank(u, 0, N)), u)
                    drained(dve, it, u)
                    tt(hsq[par], hc[par], hc[par], ALU.mult).then_inc(hsq_ready, 1)
                    u = UNIT[b, par, "V"]
                    filled(dve, it, u)
                    drain(nc.vector.tensor_copy(vb[par], bank(u, 0, D)), u)
                    drained(dve, it, u)
                    tt(vmask[par], vb[par].unsqueeze(1).broadcast_to([N, T4, D]), cm, ALU.mult)\
                        .then_inc(vmask_ready, 1)
                if b == L2_FF:
                    u = UNIT[b, par, "U0"]
                    filled(dve, it, u)
                    drained(dve, it, UNIT[b, par, "U1"])
                    for t in range(T4):
                        last = nc.vector.scalar_tensor_tensor(
                            out=hid[par][:, t, :], in0=bank(u, t * N, (t + 1) * N), scalar=v(f"ff1_2_{t}"),
                            in1=act_out[par][:, t, :], op0=ALU.add, op1=ALU.mult)
                    drain(last, u)
                if b == L3_FF:
                    u = UNIT[b, par, "U0"]
                    given(dve, it, act_ready, "act", "values", b, par)
                    drain(nc.vector.scalar_tensor_tensor(
                        out=mid[par].rearrange("p t n -> p (t n)"), in0=act_out[par].rearrange("p t n -> p (t n)"),
                        scalar=1.0, in1=bank(u), op0=ALU.add, op1=ALU.mult), u)
                    drained(dve, it, u)
                    u = UNIT[b, par, "U1"]
                    filled(dve, it, u)
                    drain(tt(hid[par].rearrange("p t n -> p (t n)"), mid[par].rearrange("p t n -> p (t n)"), bank(u),
                             ALU.mult), u)

            def scores(it, b, par):
                k = KIND[b]
                if k == "ff":
                    return
                if b == L3_SELF:
                    u = UNIT[b, par, "VAR"]
                    filled(dve, it, u)
                    drain(ts(hve[par], bank(u, 0, N), 1e-6, None, ALU.add), u)
                    given(dve, it, hrstd_ready, "head", "scores", b, par)
                    after(step(tt(hz[par], hc[par], hrs[par], ALU.mult)))
                    ts(qT[par][:, 0, :], hz[par], qn_scaled[:, 0:1], qn_scaled[:, 1:2], ALU.mult, ALU.add)
                    after(step(ts(hk[par], hz[par], v("kn_w"), v("kn_b"), ALU.mult, ALU.add)))
                    for j in range(T4):
                        last = ts(kT[par][:, j, :], hk[par], c("rowmask")[:, j:j + 1], None, ALU.mult)
                    last.then_inc(heads_ready, 1)

                def reciprocal(g):
                    drained(dve, it, UNIT[b, par, f"S{g}"])
                    hs = slice(T4 * g, T4 * g + T4)
                    nc.vector.reciprocal(rinv[par][:, hs], sums[par][:, hs]).then_inc(rinv_ready, 1)

                for g in range(4):
                    u = UNIT[b, par, f"S{g}"]
                    filled(dve, it, u)
                    nc.vector.tensor_reduce(negmax[par][:, T4 * g:T4 * g + T4],
                                            bank(u).rearrange("p (h m) -> p h m", h=T4), AX, ALU.max,
                                            negate=True).then_inc(negmax_ready, 1)
                    if g:
                        reciprocal(g - 1)
                reciprocal(3)

            def mix(it, b, par):
                k = KIND[b]
                if k != "ff":
                    for g in range(4):
                        u = UNIT[b, par, f"PT{g}"]
                        filled(dve, it, u)
                        drain(nc.vector.tensor_copy(PT[par][:, g * BANK:(g + 1) * BANK], bank(u)), u)
                u = UNIT[b, par, "D" if k == "ff" else "PJ" if k == "small" else "PV"]
                filled(dve, it, u)
                after(residual[par])
                if b == 0:
                    dve.wait_ge(ctxT_loaded[par], it * 16 + 16)
                if b < L3_SELF:
                    drain(tt(X[par][:, :], bank(u, 0, D), xb[par][:, :], ALU.add), u)
                    drained(dve, it, u)
                else:
                    i = b - L3_SELF
                    drain(nc.vector.scalar_tensor_tensor(
                        out=res[par], in0=bank(u, 0, D), scalar=0.5 if b == L3_FF else 1.0,
                        in1=gates[par][:, i * D:(i + 1) * D], op0=ALU.mult, op1=ALU.mult), u)
                    drained(dve, it, u)
                    ins = tt(X[par][:, :], res[par], xb[par][:, :], ALU.add)
                    if b == LAST:
                        ins.then_inc(out_ready, 1)
                    else:
                        after(step(ins))
                if b < LAST:
                    norm(it, par, b + 1)

            set_up()
            with dve.Fori(0, PAIRS) as it:
                turn[0] = it
                for phase, b, par in ORDER:
                    {"prelude": prelude, "project": project, "values": values, "scores": scores,
                     "mix": mix}[phase](it, b, par)
            assert steps[0] == DVE_STEPS, steps[0]


def constants():
    t = np.zeros((128, NCONST), np.float32)
    p = np.arange(128)
    t[:, CONST["ident"]] = np.eye(128)
    mean8 = (p[:, None] // HD == p[None, :] // HD) / HD
    t[:, CONST["mean8"]] = mean8
    t[:, CONST["center"]] = np.eye(128) - mean8
    member = (p[:, None] // HD) % T4 == np.arange(T4)[None, :]
    t[:, CONST["rowmask"]] = member
    t[:, CONST["colmask"]] = member.T.reshape(1, -1)
    inv = (1.0 / np.float32(10000.0) ** (np.arange(0, DH, 2, dtype=np.float32) / np.float32(DH))).astype(np.float32)
    ang = np.arange(N, dtype=np.float32)[:, None] * inv[None, :]
    cos = np.repeat(np.cos(ang), 2, axis=1)
    sin = np.stack([-np.sin(ang), np.sin(ang)], axis=-1).reshape(N, DH)
    scale = float(DH) ** -0.5
    t[:, CONST["cosk"]], t[:, CONST["sink"]] = cos, sin
    t[:, CONST["cosq"]], t[:, CONST["sinq"]] = cos * scale, sin * scale
    t[:, CONST["neghalf"]] = -0.5
    return t


def laid_out(a):
    L0, L1, L2, L3 = ({k.removeprefix(f"L{i}_xcond_"): v for k, v in a.items() if k.startswith(f"L{i}_")}
                      for i in range(4))
    down = lambda m: m.reshape(T4, 128, D).transpose(1, 0, 2)
    ada_w, ada_b = L3["adaln_w"].reshape(9, D, D), L3["adaln_b"].reshape(9, D)
    plain, gate = [0, 1, 3, 4, 6, 7], [2, 5, 8]
    t16 = lambda v: np.tile(v, H)
    vecs = [L0["ln1_w"], L0["ln1_b"], L0["ln2_w"], L0["ln2_b"], L0["g1_b"], L0["b1_b"], L0["g2_b"], L0["b2_b"]]
    vecs += list(L1["b_ada"].reshape(6, D))
    for n in ("n1_b", "n2_b", "n3_b"):
        vecs += list(L2[n].reshape(2, D))
    vecs += [ada_b[i] for i in plain] + list(L0["ff_b1"].reshape(4, D))
    vecs += [L1["b_qkv"][0:D], L1["b_qkv"][D:2 * D], L1["b_ctx"]] + list(L1["b_fc1"].reshape(4, D))
    vecs += list(L2["ff_b1"].reshape(8, D))
    vecs += [t16(L3["qn_w"]), t16(L3["qn_b"]), t16(L3["kn_w"]), t16(L3["kn_b"])]
    vecs += [L3["ca_in_b"][0:D], L3["ca_in_b"][D:2 * D], L3["cond_b"]]
    rows = [L0["sa_bo"], L0["ca_bo"], L0["ff_b2"], L1["b_proj"], L1["b_out"], L1["b_fc2"],
            L2["o1_b"], L2["o2_b"], L2["ff_b2"], L3["ca_out_b"], L1["b_qkv"][2 * D:], L3["ca_in_b"][2 * D:]]
    rows += [ada_b[i] for i in gate]
    w = {"wq0": L0["sa_wq"], "wk0": L0["sa_wkv"][:, :MID], "cq0": L0["ca_wq"], "ck0": L0["ca_wkv"][:, :MID],
         "f10": L0["ff_w1"], "f20": down(L0["ff_w2"]),
         "qkv1": L1["W_qkv"], "proj1": L1["W_proj"], "ctx1": L1["W_ctx"],
         "cqkv1": np.concatenate([L1["W_q"], L1["W_k"], L1["W_v"]], axis=1), "out1": L1["W_out"],
         "f11": L1["W_fc1"], "f21": down(L1["W_fc2"]),
         "wq2": L2["q1"], "wk2": L2["k1"], "cq2": L2["q2"], "ck2": L2["k2"], "f12": L2["ff_w1"], "f22": down(L2["ff_w2"]),
         "gate3": np.concatenate([ada_w[i].T for i in gate], axis=1), "cond3": L3["cond_w"].T,
         "cqkv3": L3["ca_in_w"].T, "out3": L3["ca_out_w"].T,
         "f13": np.concatenate([L3["w1"].T, L3["w3"].T], axis=1), "f23": down(L3["w2"].T)}
    setup_w = {"vt_sa0": L0["sa_wkv"][:, MID:].T, "wo_sa0": L0["sa_wo"],
               "vt_ca0": L0["ca_wkv"][:, MID:].T, "wo_ca0": L0["ca_wo"],
               "vt_sa2": L2["v1"].T, "wo_sa2": L2["o1_w"], "vt_ca2": L2["v2"].T, "wo_ca2": L2["o2_w"],
               "mod_lin": np.concatenate([L0["g1_w"], L0["b1_w"], L0["g2_w"], L0["b2_w"],
                                          L2["n1_w"], L2["n2_w"], L2["n3_w"]], axis=1),
               "mod_silu": np.concatenate([L1["W_ada"]] + [ada_w[i].T for i in plain], axis=1)}
    main = {"x": a["x"], "ctx": a["ctx_768"], "ctx_t": a["ctx_768"].transpose(0, 2, 1), "cond_t": a["cond_1024"].T,
            "vecs": np.stack(vecs, axis=1), "lnc": np.stack([L0["ca_lnc_w"], L0["ca_lnc_b"]], axis=1),
            "rows": np.concatenate(rows), "consts": constants()}
    return main, setup_w, w


def kernel(**inputs):
    import concourse.bacc as bacc
    from concourse.bass_utils import run_bass_kernel_spmd

    nc = bacc.Bacc("TRN2", target_bir_lowering=False, num_devices=1)
    main, setup_w, w = laid_out({k: np.asarray(v) for k, v in inputs.items()})
    arrays = {}

    def declare(group, prefix):
        aps = {}
        for name, a in group.items():
            a = np.ascontiguousarray(a)
            arrays[prefix + name] = a
            aps[name] = nc.dram_tensor(prefix + name, a.shape, mybir.dt.from_np(a.dtype), kind="ExternalInput").ap()
        return aps

    m, s, r = declare(main, "in_"), declare(setup_w, "set_"), declare({n: w[n] for n in WEIGHTS}, "res_")
    out = nc.dram_tensor("out_x", (S, N, D), mybir.dt.float32, kind="ExternalOutput").ap()
    build(nc, m["x"], m["ctx"], m["ctx_t"], m["cond_t"], m["vecs"], m["lnc"], m["rows"], m["consts"], s, r, out)
    return run_bass_kernel_spmd(nc, [arrays], core_ids=[0]).results[0]["out_x"]
```

```python
import concourse.bass as bass
from concourse import mybir
from contextlib import ExitStack
import numpy as np

S, N, D, CD = 16, 128, 128, 96
H, DH, HD = 16, 64, 8
MID = H * DH
PAIRS = S // 2
BANKS, BANK = 8, 512
T4 = 4

KIND = ["rope", "rope", "ff", "small", "small", "ff", "flat", "flat", "ff", "small", "small", "ff"]
CROSS = [False, True, False] * 4
LAST = len(KIND) - 1
EPS = [1e-5] * 3 + [1e-6] * 3 + [1e-5] * 3 + [1e-6] * 3
EPS_CTX = 1e-5
EPS_HEAD = 1e-6
MODPAIR = [0, 0, 1, 2, 3, 4, 5, 6, 7, 8, 9, 10]
NMOD = 11
L3_SELF, L3_CROSS, L3_FF = 9, 10, 11
L2_FF = 8

VEC = {n: i for i, n in enumerate(
    ["ln1_w", "ln1_b", "ln2_w", "ln2_b"]
    + [f"raw{i}" for i in range(22)]
    + [f"ff1_0_{t}" for t in range(4)] + ["bq1", "bk1", "bctx"] + [f"fc1_{t}" for t in range(4)]
    + [f"ff1_2_{t}" for t in range(8)] + ["qn_w", "qn_b", "kn_w", "kn_b", "bq3", "bk3", "bcond"])}
ROW = {n: i for i, n in enumerate(
    ["o0", "o1", "o2", "o3", "o4", "o5", "o6", "o7", "o8", "o10", "bv1", "bv3", "g0", "g1", "g2"])}
OUT_ROW = ["o0", "o1", "o2", "o3", "o4", "o5", "o6", "o7", "o8", None, "o10", None]
CONST, _c = {}, 0
for _n, _w in [("ident", 128), ("center", 128), ("mean8", 128), ("rowmask", 4), ("groupmask", 4), ("colmask", 512),
               ("cosq", 64), ("sinq", 64), ("cosk", 64), ("sink", 64), ("neghalf", 1)]:
    CONST[_n] = slice(_c, _c + _w)
    _c += _w
NCONST = _c


RING = 6
HOP = 0.2
TABLE_LOAD = 1.3
LEAD = 7.5
PE, DVE, ACTE, POOL = "TensorE", "VectorE", "ScalarE", "GpSimd"


def steps_of(b, par):
    k = KIND[b]
    out = []

    def add(engine, step, cost, *after):
        out.append(((engine, step, b, par), cost, [a if len(a) == 4 else (*a, b, par) for a in after]))

    add(DVE, "stats", 0.85 if b else 1.4, (DVE, "sum", b - 1 if b else LAST, par))
    add(POOL, "power", 0.5 if b else 1.0, (DVE, "stats"))
    add(DVE, "norm", 0.3 if b else 0.6, (POOL, "power"))
    if b == 0:
        add(DVE, "mods", 0.2)
    add(PE, "T", 0.12, *([(DVE, "norm")] if b else []))
    add(DVE, "T", 0.32, (PE, "T"), *([] if b else [(DVE, "mods")]))
    if k in ("rope", "flat"):
        source = (DVE, "T")
        if k == "rope" and CROSS[b]:
            add(PE, "CT", 0.15, (PE, "T"))
            add(DVE, "CT", 0.25, (PE, "CT"))
            source = (DVE, "CT")
        for n in ("Q0", "K0", "Q1", "K1"):
            add(PE, n, 0.9, (DVE, "T"), *([source] if n[0] == "K" else []))
            if k == "rope":
                add(DVE, n, 1.25, (PE, n))
                add(POOL, "R" + n, 1.2, (DVE, n))
                add(PE, n[0] + "T" + n[1], 0.45, (POOL, "R" + n))
                add(ACTE, n[0] + "T" + n[1], 0.55, (PE, n[0] + "T" + n[1]))
            else:
                add(DVE, n, 0.6, (PE, n))
        for i in range(4):
            add(PE, f"VW{i}", 0.9, source, (DVE, "T"))
            add(ACTE, f"VW{i}", 0.5, (PE, f"VW{i}"))
        for i in range(2):
            q = [(ACTE, f"{n}T{i}") if k == "rope" else (DVE, f"{n}{i}") for n in "QK"]
            add(PE, f"S{2 * i}", 1.75, *q)
    elif k == "small":
        if b == L3_SELF:
            add(PE, "HC", 0.25, (DVE, "T"))
            add(DVE, "HC", 0.55, (PE, "HC"))
            add(PE, "VAR", 0.25, (DVE, "HC"))
            add(DVE, "heads", 6.0, (PE, "VAR"))
            add(PE, "G", 0.9, (PE, "T"))
            add(DVE, "G", 0.5, (PE, "G"))
            add(PE, "V", 0.15, (DVE, "T"))
            ready = (DVE, "heads")
        else:
            source = (DVE, "T")
            if CROSS[b]:
                add(PE, "C", 0.25, (DVE, "T", b - 1, par))
                add(DVE, "C", 0.25, (PE, "C"))
                source = (DVE, "C")
            add(PE, "K", 0.25, (DVE, "T"), source)
            add(DVE, "K", 0.9, (PE, "K"))
            add(PE, "Q", 0.25, (DVE, "T"))
            add(ACTE, "Q", 1.2, (PE, "Q"))
            add(PE, "V", 0.25, (DVE, "T"), source)
            ready = (DVE, "K")
        add(DVE, "V", 0.9, (PE, "V"))
        for g in range(4):
            add(PE, f"S{g}", 0.9, ready, *([] if b == L3_SELF else [(ACTE, "Q")]))
    if k == "ff":
        add(PE, "U0", 0.9, (DVE, "T"))
        if b >= L2_FF:
            add(PE, "U1", 0.9, (DVE, "T"))
        if b < L2_FF:
            add(ACTE, "U0", 1.3, (PE, "U0"))
            hidden = (ACTE, "U0")
        elif b == L2_FF:
            add(ACTE, "U1", 1.3, (PE, "U1"))
            add(DVE, "U0", 1.0, (PE, "U0"), (ACTE, "U1"))
            hidden = (DVE, "U0")
        else:
            add(ACTE, "U0", 0.6, (PE, "U0"))
            add(DVE, "U0", 0.65, (ACTE, "U0"))
            add(DVE, "U1", 0.65, (DVE, "U0"), (PE, "U1"))
            hidden = (DVE, "U1")
        add(PE, "D", 0.9, hidden)
        add(DVE, "sum", 0.35, (PE, "D"))
        return out
    for g in range(4):
        s = f"S{g // 2 * 2}" if k != "small" else f"S{g}"
        add(DVE, f"max{g}", 0.6, (PE, s))
        add(ACTE, f"exp{g}", 1.4, (DVE, f"max{g}"))
        add(DVE, f"rcp{g}", 0.12, (ACTE, f"exp{g}"))
        add(POOL, f"prob{g}", 1.0, (DVE, f"rcp{g}"))
        add(PE, f"PT{g}", 0.45, (POOL, f"prob{g}"), *([(PE, ["QT0", "QT1", "KT0", "KT1"][g])] if k == "rope" else []))
        add(DVE, f"PT{g}", 0.6, (PE, f"PT{g}"))
        values = (DVE, "V") if k == "small" else (ACTE, f"VW{g}")
        add(PE, f"MX{g}", 0.45 if k == "small" else 0.9, (DVE, f"PT{g}"), values, *([(PE, f"MX{g - 1}")] if g else []))
    if k == "small":
        add(DVE, "PV", 0.25, (PE, "MX3"))
        add(PE, "PJ", 0.25, (DVE, "PV"))
        add(DVE, "sum", 0.35, (PE, "PJ"))
    else:
        add(DVE, "sum", 0.35, (PE, "MX3"))
    return out


def units_of(key):
    _, step, b, par = key
    if step[0] == "S" and KIND[b] != "small":
        return [step, f"S{int(step[1]) + 1}"]
    if step[:2] == "MX":
        return ["PV"] if step == "MX0" else []
    return [step]


def unit_read(key):
    engine, step, b, par = key
    if engine in (PE, POOL) or step in ("stats", "norm", "mods") or step[:3] in ("max", "rcp"):
        return None
    if step[:3] == "exp":
        return "S" + step[3]
    if step == "heads":
        return "VAR"
    if step == "sum":
        return "D" if KIND[b] == "ff" else "PJ" if KIND[b] == "small" else "PV"
    if engine == ACTE and b == L3_FF:
        return None
    return step


def table_of(key):
    engine, step, b, _ = key
    if engine != ACTE or step[0] not in "eU":
        return None
    return {2: "gelu", 5: "gelu_tanh", 8: "gelu"}.get(b, "exp")


def schedule():
    cost, after, users, way = {}, {}, {}, {}
    for par in range(2):
        for b in range(LAST + 1):
            for key, c, a in steps_of(b, par):
                cost[key], after[key] = c, a
    for key in after:
        for a in after[key]:
            users.setdefault(a, []).append(key)

    def length(key):
        if key not in way:
            way[key] = cost[key] + max([length(u) + HOP for u in users.get(key, [])], default=0)
        return way[key]

    order = {e: [] for e in (PE, DVE, ACTE, POOL)}
    free = {e: 0.0 for e in order}
    vacant = {i: 0.0 for i in range(BANKS)}
    end, bank_of, roped, table = {}, {}, [], "exp"
    left = {key: len(after[key]) for key in cost}
    while left:
        best = None
        for key, missing in left.items():
            if missing:
                continue
            e, step, b, par = key
            start = max([free[e]] + [end[a] + (HOP if a[0] != e else 0) for a in after[key]])
            banks, units = [], units_of(key) if e == PE else []
            if units:
                own = units[0] in ("PV", "PJ", "D")
                banks = [RING + par] if own else [i for i in range(RING) if vacant[i] is not None]
                banks = sorted(banks, key=lambda i: (vacant[i] or 0, i))[:len(units)]
                if len(banks) < len(units) or vacant[banks[-1]] is None:
                    continue
                start = max(start, vacant[banks[-1]])
            if is_rope_product(key) and len(roped) >= 2:
                _, old, old_b, old_par = roped[-2]
                added = (POOL, "R" + old, old_b, old_par)
                if added not in end:
                    continue
                start = max(start, end[added] + HOP)
            score = (start, -length(key) - (LEAD if par == 0 else 0), key)
            if best is None or score < best[0]:
                best = (score, key, start, banks)
        _, key, start, banks = best
        e, _, b, par = key
        switch = table_of(key) not in (None, table)
        table = table_of(key) or table
        end[key] = free[e] = start + cost[key] + (TABLE_LOAD if switch else 0)
        order[e].append(key)
        del left[key]
        for unit, i in zip(units_of(key) if e == PE else [], banks):
            bank_of[b, par, unit] = i
            vacant[i] = None
        unit = unit_read(key)
        if unit is not None:
            vacant[bank_of[b, par, unit]] = end[key] + HOP
        if is_rope_product(key):
            roped.append(key)
        for user in users.get(key, []):
            left[user] -= 1
    return order, bank_of


def is_rope_product(key):
    return key[0] == DVE and KIND[key[2]] == "rope" and key[1] in ("Q0", "Q1", "K0", "K1")


ORDER, BANK_OF = schedule()

UNIT, PER_TURN = {}, [0] * BANKS
for _key in ORDER[PE]:
    for _n in units_of(_key):
        _bank = BANK_OF[_key[2], _key[3], _n]
        UNIT[_key[2], _key[3], _n] = (_bank, PER_TURN[_bank])
        PER_TURN[_bank] += 1
SETUP_UNITS = 17
SETUP = [(SETUP_UNITS - b + BANKS - 1) // BANKS for b in range(BANKS)]


def signals_of(engine, step, b):
    if step in ("stats", "power", "norm"):
        return {step: 1} if b else {}
    if step == "mods":
        return {}
    if step[:3] in ("max", "rcp"):
        return {step[:3]: 1}
    if engine == POOL:
        return {"prob" if step[0] == "p" else "rotated": 1}
    if engine == DVE and step == "HC":
        return {"squares": 1}
    if step == "heads":
        return {"heads": 1}
    if engine == DVE and step == "V":
        return {"values": 1}
    if engine == ACTE and step == "U0" and b == L3_FF:
        return {"tanh": 1}
    return {}


AT, TOTAL = {}, {}
for _engine in ORDER:
    for _, _step, _b, _par in ORDER[_engine]:
        for _n, _k in signals_of(_engine, _step, _b).items():
            TOTAL[_n] = TOTAL.get(_n, 0) + _k
            AT[_n, _step, _b, _par] = TOTAL[_n]

ROPE = [_key for _key in ORDER[DVE] if is_rope_product(_key)]

DVE_STEPS = 110

WEIGHTS = ["wq0", "wk0", "cq0", "ck0", "f10", "f20",
           "qkv1", "proj1", "ctx1", "cqkv1", "out1", "f11", "f21",
           "wq2", "wk2", "cq2", "ck2", "f12", "f22",
           "gate3", "cond3", "cqkv3", "out3", "f13", "f23"]
LAYER_OF = {n: int(n[-1]) for n in WEIGHTS}
LAYER_COUNT = [sum(l == i for l in LAYER_OF.values()) for i in range(4)]


def tile_of(g, j):
    return DH * (g % 2), T4 * (g // 2) + j


def build(nc, x, ctx, ctx_t, cond_t, vecs, lnc, rows, consts, setup_w, w, out):
    fp32 = mybir.dt.float32
    int32 = mybir.dt.int32
    ALU = mybir.AluOpType
    ACT = mybir.ActivationFunctionType
    AX = mybir.AxisListType.X
    stack = ExitStack()
    with stack:
        def sb(name, *shape):
            return stack.enter_context(nc.sbuf_tensor(name, list(shape), fp32))

        def sem(name):
            return stack.enter_context(nc.semaphore(name))

        W = {n: sb("w_" + n, *a.shape) for n, a in w.items()}
        M = {n: sb("m_" + n, r, H * D) for n, r in (("sa0", D), ("ca0", CD), ("sa2", D), ("ca2", CD))}
        C = sb("consts", 128, NCONST)
        V = sb("vecs", 128, len(VEC))
        LNC = sb("lnc", CD, 2)
        R = sb("rows", 128, len(ROW) * D)
        mod = sb("mod", 128, S, 2 * NMOD)
        condT = sb("condT", 128, S)
        siluT = sb("siluT", 128, S)
        silu_t = sb("silu_t", 128, 2 * S)
        raw = sb("raw", 128, 2 * NMOD, S)
        qn_masked = sb("qn_masked", 128, 2, T4)
        qbias = {b: sb(f"qbias{b}", 128, T4) for b in (3, 10)}
        qscale = sb("qscale", 128, T4)
        prod = sb("prod", 128, 2, 2, BANK)

        def pair(name, *shape):
            return [sb(f"{name}{p}", *shape) for p in range(2)]

        xin = pair("xin", N, D)
        cin = pair("cin", N, CD)
        ctxT = pair("ctxT", CD, N)
        X = pair("X", N, D)
        xb = pair("xb", N, D)
        gb = pair("gb", N, D)
        xn = pair("xn", N, D)
        cn = pair("cn", N, CD)
        hT = pair("hT", D, N)
        kvT = pair("kvT", D, N)
        modc = pair("modc", 128, 2 * NMOD)
        cb = pair("cb", 128, N)
        gates = pair("gates", N, 3 * D)
        st = pair("st", 128, 2, 6)
        mv = pair("mv", 128, 2, 2)
        ve = pair("ve", 128, 2)
        rstd = pair("rstd", 128, 2)
        negmax = pair("negmax", N, H)
        sums = pair("sums", N, H)
        rinv = pair("rinv", N, H)
        outT = pair("outT", D, N)
        qT = pair("qT", 128, H // 2, N)
        kT = pair("kT", 128, H // 2, N)
        VW = pair("VW", N, H * D)
        E = pair("E", N, H, N)
        PT = pair("PT", N, H * N)
        rot = [PT[p][:, :].rearrange("p (s c) -> p s c", s=2) for p in range(2)]
        vb = [VW[p][:, 512:512 + D] for p in range(2)]
        vmask = [VW[p][:, 0:T4 * D].rearrange("p (j f) -> p j f", j=T4) for p in range(2)]
        hc = [VW[p][:, 1024:1024 + N] for p in range(2)]
        hsq = [VW[p][:, 1152:1152 + N] for p in range(2)]
        hve = [VW[p][:, 1280:1280 + N] for p in range(2)]
        hrs = [VW[p][:, 1408:1408 + N] for p in range(2)]
        hz = [VW[p][:, 1536:1536 + N] for p in range(2)]
        hk = [VW[p][:, 1664:1664 + N] for p in range(2)]
        res = [VW[p][:, 1792:1792 + D] for p in range(2)]
        hid = [E[p][:, 0:T4, :] for p in range(2)]
        act_out = [E[p][:, T4:2 * T4, :] for p in range(2)]
        mid = [E[p][:, 2 * T4:3 * T4, :] for p in range(2)]

        stage = {}
        for n, src in setup_w.items():
            stage[n] = {"vt_sa0": E[0][:, 0:8, :], "wo_sa0": E[0][:, 8:16, :],
                        "vt_sa2": PT[0][:, 0:1024].rearrange("p (t i) -> p t i", t=8),
                        "wo_sa2": PT[0][:, 1024:2048].rearrange("p (t i) -> p t i", t=8),
                        "vt_ca0": VW[0][:, 0:768].rearrange("p (t i) -> p t i", t=8),
                        "wo_ca0": VW[0][:, 1024:2048].rearrange("p (t i) -> p t i", t=8),
                        "vt_ca2": E[1][:, 0:6, :].rearrange("p a b -> p (a b)").rearrange("p (t i) -> p t i", t=8),
                        "wo_ca2": E[1][:, 8:16, :],
                        "mod_lin": PT[1][:, 0:10 * D],
                        "mod_silu": VW[1][:, 0:12 * D]}[n]

        ps = stack.enter_context(nc.psum_tensor("ps", [128, BANKS, BANK], fp32))

        bank_full = [sem(f"bank_full{b}") for b in range(BANKS)]
        bank_drained = [sem(f"bank_drained{b}") for b in range(BANKS)]
        small_loaded = sem("small_loaded")
        setup_loaded = {n: sem("setup_loaded_" + n) for n in ("sa0", "ca0", "sa2", "ca2", "mod")}
        layer_loaded = [sem(f"layer_loaded{i}") for i in range(4)]
        x_loaded = [sem(f"x_loaded{p}") for p in range(2)]
        ctxT_loaded = [sem(f"ctxT_loaded{p}") for p in range(2)]
        silu_in = sem("silu_in")
        silu_ready = sem("silu_ready")
        setup_step = sem("setup_step")
        signal = {n: sem(n + "_ready") for n in (
            "stats",
            "power",
            "norm",
            "rotated",
            "max",
            "rcp",
            "prob",
            "squares",
            "heads",
            "values",
            "tanh")}
        first = {n: [sem(f"first_{n}{p}") for p in range(2)] for n in ("stats", "power", "norm")}
        dve_step = sem("dve_step")
        q_constants = sem("q_constants")
        out_ready = [sem(f"out_ready{p}") for p in range(2)]
        out_done = [sem(f"out_done{p}") for p in range(2)]

        def bank(u, a=0, b=BANK):
            return ps[:, u[0], a:b]

        def c(name):
            return C[:, CONST[name]]

        def v(name):
            return V[:, VEC[name]:VEC[name] + 1]

        def row(name, n=1):
            return R[:, ROW[name] * D:(ROW[name] + n) * D]

        def written(u):
            return SETUP[u[0]] + u[1] + 1

        def vacant(u):
            return SETUP[u[0]] + u[1]

        def latest_first(*units):
            return sorted(units, reverse=True)

        waited = {}

        def fresh(eng, semaphore, count):
            covered = waited.get((eng, semaphore.name), 0) >= count
            if not covered:
                waited[eng, semaphore.name] = count
            return not covered

        block = stack.enter_context(nc.Block())

        @block.sync
        def _(sp):
            def at(dram, i):
                return dram[bass.ds(i, 1)].rearrange("a n d -> (a n) d")

            sp.dma_start(condT[:, :], cond_t).then_inc(small_loaded, 16)
            sp.dma_start(V[:, :], vecs).then_inc(small_loaded, 16)
            sp.dma_start(stage["mod_lin"], setup_w["mod_lin"]).then_inc(setup_loaded["mod"], 16)
            sp.dma_start(stage["mod_silu"], setup_w["mod_silu"]).then_inc(setup_loaded["mod"], 16)
            for n in ("sa0", "ca0", "sa2", "ca2"):
                for k in ("vt_", "wo_"):
                    sp.dma_start(stage[k + n], setup_w[k + n].rearrange("(t p) i -> p t i", t=8))\
                      .then_inc(setup_loaded[n], 16)
                if n == "sa0":
                    sp.dma_start(C[:, :], consts).then_inc(small_loaded, 16)
                    sp.dma_start(LNC[:, :], lnc).then_inc(small_loaded, 16)
                    sp.dma_start(R[:, :], rows.partition_broadcast(128)).then_inc(small_loaded, 16)
                    for p in range(2):
                        sp.dma_start(xin[p][:, :], x[p]).then_inc(x_loaded[p], 16)
                        sp.dma_start(cin[p][:, :], ctx[p]).then_inc(x_loaded[p], 16)
            for n in W:
                sp.dma_start(W[n][:], w[n]).then_inc(layer_loaded[LAYER_OF[n]], 16)
            for p in range(2):
                sp.dma_start(ctxT[p][:, :], ctx_t[p]).then_inc(ctxT_loaded[p], 16)
            with sp.Fori(0, PAIRS - 1) as it:
                normed = sp.snap(it * 2 + 2)
                stored = sp.snap(it * 16 + 16)
                produced = sp.snap(it + 1)
                this = [it * 2 + p for p in range(2)]
                following = [it * 2 + (2 + p) for p in range(2)]
                for p in range(2):
                    sp.wait_ge(first["norm"][p], normed)
                    sp.dma_start(xin[p][:, :], at(x, following[p])).then_inc(x_loaded[p], 16)
                    sp.dma_start(cin[p][:, :], at(ctx, following[p])).then_inc(x_loaded[p], 16)
                for p in range(2):
                    sp.wait_ge(out_ready[p], produced)
                    sp.dma_start(at(out, this[p]), X[p][:, :]).then_inc(out_done[p], 16)
                for p in range(2):
                    sp.wait_ge(out_done[p], stored)
                    sp.dma_start(ctxT[p][:, :], at(ctx_t, following[p])).then_inc(ctxT_loaded[p], 16)
            for p in range(2):
                sp.wait_ge(first["norm"][p], 2 * PAIRS)
                sp.dma_start(xin[p][:, :], x[p]).then_inc(x_loaded[p], 16)
                sp.dma_start(cin[p][:, :], ctx[p]).then_inc(x_loaded[p], 16)
            for p in range(2):
                sp.wait_ge(out_ready[p], PAIRS)
                sp.dma_start(out[S - 2 + p], X[p][:, :]).then_inc(out_done[p], 16)
            for p in range(2):
                sp.wait_ge(out_done[p], 16 * PAIRS)

        @block.tensor
        def _(pe):
            mm = nc.tensor.matmul

            def set_up():
                pe.wait_ge(small_loaded, 16 * 5)
                pe.wait_ge(setup_loaded["mod"], 32)
                pe.wait_ge(silu_ready, 1)
                lin = silu = 0
                for i in range(22):
                    if i < 4 or 10 <= i < 16:
                        lhs, rhs, lin = stage["mod_lin"][:, lin * D:(lin + 1) * D], condT, lin + 1
                    else:
                        lhs, rhs, silu = stage["mod_silu"][:, silu * D:(silu + 1) * D], siluT, silu + 1
                    last = mm(ps[:, 0, i * S:(i + 1) * S], lhs, rhs[:, :], start=True, stop=True)
                last.then_inc(bank_full[0], 1)
                u = 1
                for n in ("sa0", "ca0", "sa2", "ca2"):
                    pe.wait_ge(setup_loaded[n], 32)
                    rows_ = M[n].shape[0]
                    for g in (0, 2):
                        for i in range(2):
                            if u + i >= BANKS:
                                pe.wait_ge(bank_drained[(u + i) % BANKS], (u + i) // BANKS)
                        for j in range(T4):
                            for i in range(2):
                                p0, t = tile_of(g + i, j)
                                last = mm(ps[0:rows_, (u + i) % BANKS, j * D:(j + 1) * D],
                                          stage["vt_" + n][p0:p0 + DH, t, :], stage["wo_" + n][p0:p0 + DH, t, :],
                                          start=True, stop=True)
                                if j == T4 - 1:
                                    last.then_inc(bank_full[(u + i) % BANKS], 1)
                        u += 2

            def step_of(it, step, b, par):
                k = KIND[b]
                wide = "c" if CROSS[b] else "w"
                units = [UNIT[b, par, n] for n in units_of((PE, step, b, par))]
                u = units[0] if units else None
                for unit in units:
                    if fresh(pe, bank_drained[unit[0]], vacant(unit)):
                        pe.wait_ge(bank_drained[unit[0]], it * PER_TURN[unit[0]] + vacant(unit))

                if step == "T":
                    if b == 0:
                        pe.wait_ge(first["norm"][par], it * 2 + 1)
                    elif fresh(pe, signal["norm"], AT["norm", "norm", b, par]):
                        pe.wait_ge(signal["norm"], it * TOTAL["norm"] + AT["norm", "norm", b, par])
                    nc.tensor.transpose(bank(u, 0, N), xn[par][:, :], c("ident")).then_inc(bank_full[u[0]], 1)
                    if b % 3 == 0 and par == first_par[b]:
                        pe.wait_ge(layer_loaded[b // 3], 16 * LAYER_COUNT[b // 3])
                elif step == "CT":
                    pe.wait_ge(first["norm"][par], it * 2 + 2)
                    nc.tensor.transpose(ps[0:CD, u[0], 0:N], cn[par][:, :], c("ident")).then_inc(bank_full[u[0]], 1)
                elif step == "C":
                    t = UNIT[b - 1, par, "T"]
                    if fresh(pe, bank_drained[t[0]], written(t)):
                        pe.wait_ge(bank_drained[t[0]], it * PER_TURN[t[0]] + written(t))
                    pe.wait_ge(ctxT_loaded[par], it * 16 + 16)
                    mm(bank(u, 0, N), W["ctx1" if b == 4 else "cond3"][:, :], ctxT[par][:, :],
                            start=True, stop=True).then_inc(bank_full[u[0]], 1)
                elif step == "G":
                    mm(bank(u, 0, 3 * D), cb[par][:, :], W["gate3"][:, :], start=True, stop=True).then_inc(bank_full[u[0]], 1)
                elif step in ("Q0", "Q1", "K0", "K1"):
                    k_of_context = step[0] == "K" and k == "rope" and CROSS[b]
                    for t in latest_first(*[UNIT[b, par, n] for n in (["T", "CT"] if k_of_context else ["T"])]):
                        if fresh(pe, bank_drained[t[0]], written(t)):
                            pe.wait_ge(bank_drained[t[0]], it * PER_TURN[t[0]] + written(t))
                    i = int(step[1])
                    if k == "rope":
                        src = kvT[par][0:CD, :] if k_of_context else hT[par][:, :]
                        mm(bank(u), src, W[wide + step[0].lower() + "0"][:, i * BANK:(i + 1) * BANK],
                                start=True, stop=True).then_inc(bank_full[u[0]], 1)
                    else:
                        src = ctxT[par][:, :] if step[0] == "K" and CROSS[b] else hT[par][:, :]
                        wt = W[wide + step[0].lower() + "2"]
                        for j in range(T4):
                            t = T4 * i + j
                            last = mm(bank(u, j * N, (j + 1) * N), wt[:, t * 128:(t + 1) * 128], src,
                                      start=True, stop=True)
                        last.then_inc(bank_full[u[0]], 1)
                elif step[:2] == "VW":
                    i = int(step[2])
                    if not CROSS[b]:
                        src, m = hT[par][:, :], M["sa0" if b == 0 else "sa2"]
                    elif k == "rope":
                        src, m = kvT[par][0:CD, :], M["ca0"]
                    else:
                        src, m = ctxT[par][:, :], M["ca2"]
                    for t in latest_first(*[UNIT[b, par, n] for n in (["T", "CT"] if k == "rope" and CROSS[b] else ["T"])]):
                        if fresh(pe, bank_drained[t[0]], written(t)):
                            pe.wait_ge(bank_drained[t[0]], it * PER_TURN[t[0]] + written(t))
                    mm(bank(u), src, m[:, i * BANK:(i + 1) * BANK], start=True, stop=True).then_inc(bank_full[u[0]], 1)
                elif step in ("U0", "U1"):
                    t = UNIT[b, par, "T"]
                    if fresh(pe, bank_drained[t[0]], written(t)):
                        pe.wait_ge(bank_drained[t[0]], it * PER_TURN[t[0]] + written(t))
                    w1 = W[f"f1{b // 3}"]
                    for j in range(T4):
                        t = T4 * int(step[1]) + j
                        last = mm(bank(u, j * N, (j + 1) * N), w1[:, t * 128:(t + 1) * 128], hT[par][:, :],
                                  start=True, stop=True)
                    last.then_inc(bank_full[u[0]], 1)
                elif step == "HC":
                    t = UNIT[b, par, "T"]
                    if fresh(pe, bank_drained[t[0]], written(t)):
                        pe.wait_ge(bank_drained[t[0]], it * PER_TURN[t[0]] + written(t))
                    mm(bank(u, 0, N), c("center"), hT[par][:, :], start=True, stop=True).then_inc(bank_full[u[0]], 1)
                elif step == "VAR":
                    count = AT["squares", "HC", b, par]
                    if fresh(pe, signal["squares"], count):
                        pe.wait_ge(signal["squares"], it * TOTAL["squares"] + count)
                    mm(bank(u, 0, N), c("mean8"), hsq[par], start=True, stop=True).then_inc(bank_full[u[0]], 1)
                elif step in ("Q", "K", "V"):
                    for t in latest_first(*[UNIT[b, par, n]
                                            for n in (["T", "C"] if CROSS[b] and step != "Q" else ["T"])]):
                        if fresh(pe, bank_drained[t[0]], written(t)):
                            pe.wait_ge(bank_drained[t[0]], it * PER_TURN[t[0]] + written(t))
                    src = kvT[par] if CROSS[b] and step != "Q" else hT[par]
                    if b == L3_SELF:
                        nc.tensor.transpose(bank(u, 0, D), hT[par][:, :], c("ident")).then_inc(bank_full[u[0]], 1)
                    else:
                        wt = W[{3: "qkv1", 4: "cqkv1", 10: "cqkv3"}[b]]
                        if step == "V":
                            mm(bank(u, 0, D), src[:, :], wt[:, 2 * D:3 * D], start=True, stop=True)\
                                .then_inc(bank_full[u[0]], 1)
                        else:
                            i = "QK".index(step)
                            mm(bank(u, 0, N), wt[:, i * D:(i + 1) * D], src[:, :], start=True, stop=True)\
                                .then_inc(bank_full[u[0]], 1)
                elif step[:2] in ("QT", "KT"):
                    count = AT["rotated", "R" + step[0] + step[2], b, par]
                    if fresh(pe, signal["rotated"], count):
                        pe.wait_ge(signal["rotated"], it * TOTAL["rotated"] + count)
                    for j in range(T4):
                        a = int(step[2]) * BANK + j * 128
                        last = nc.tensor.transpose(bank(u, j * N, (j + 1) * N),
                                                   rot[par][:, "QK".index(step[0]), a:a + 128], c("ident"))
                    last.then_inc(bank_full[u[0]], 1)
                elif step[0] == "S" and k == "small":
                    g = int(step[1])
                    if b == L3_SELF:
                        count = AT["heads", "heads", b, par]
                        if fresh(pe, signal["heads"], count):
                            pe.wait_ge(signal["heads"], it * TOTAL["heads"] + count)
                    else:
                        for t in latest_first(UNIT[b, par, "Q"], UNIT[b, par, "K"]):
                            if fresh(pe, bank_drained[t[0]], written(t)):
                                pe.wait_ge(bank_drained[t[0]], it * PER_TURN[t[0]] + written(t))
                    mm(bank(u), qT[par][:, g, :], kT[par][:, 0:T4, :], start=True, stop=True)\
                        .then_inc(bank_full[u[0]], 1)
                elif step[0] == "S":
                    g = int(step[1])
                    turned = "T" if k == "rope" else ""
                    for t in latest_first(*[UNIT[b, par, f"{n}{turned}{g // 2}"] for n in "QK"]):
                        if fresh(pe, bank_drained[t[0]], written(t)):
                            pe.wait_ge(bank_drained[t[0]], it * PER_TURN[t[0]] + written(t))
                    for j in range(T4):
                        for i, unit in enumerate(units):
                            p0, t = tile_of(g + i, j)
                            last = mm(bank(unit, j * N, (j + 1) * N), qT[par][p0:p0 + DH, t, :],
                                      kT[par][p0:p0 + DH, t, :], start=True, stop=True)
                            if j == T4 - 1:
                                last.then_inc(bank_full[unit[0]], 1)
                elif step[:2] == "PT":
                    g = int(step[2])
                    count = AT["prob", f"prob{g}", b, par]
                    if fresh(pe, signal["prob"], count):
                        pe.wait_ge(signal["prob"], it * TOTAL["prob"] + count)
                    for j in range(T4):
                        last = nc.tensor.transpose(bank(u, j * N, (j + 1) * N), E[par][:, T4 * g + j, :], c("ident"))
                    last.then_inc(bank_full[u[0]], 1)
                elif step[:2] == "MX":
                    g = int(step[2])
                    if k == "small":
                        count = AT["values", "V", b, par]
                        if fresh(pe, signal["values"], count):
                            pe.wait_ge(signal["values"], it * TOTAL["values"] + count)
                    for t in latest_first(*[UNIT[b, par, f"{n}{g}"] for n in (["PT"] if k == "small" else ["PT", "VW"])]):
                        if fresh(pe, bank_drained[t[0]], written(t)):
                            pe.wait_ge(bank_drained[t[0]], it * PER_TURN[t[0]] + written(t))
                    u = UNIT[b, par, "PV"]
                    for j in range(T4):
                        h = T4 * g + j
                        pt = PT[par][:, h * N:(h + 1) * N]
                        if k == "small":
                            p0 = 32 * g
                            last = mm(ps[p0:p0 + 32, u[0], 0:N], vmask[par][:, j, p0:p0 + 32], pt,
                                      start=(j == 0), stop=(j == T4 - 1), tile_position=(0, p0))
                        else:
                            last = mm(bank(u, 0, D), pt, VW[par][:, h * D:(h + 1) * D],
                                      start=(h == 0), stop=(h == H - 1))
                    if g == 3:
                        last.then_inc(bank_full[u[0]], 1)
                elif step == "D":
                    t = UNIT[b, par, "U1" if b == L3_FF else "U0"]
                    if fresh(pe, bank_drained[t[0]], written(t)):
                        pe.wait_ge(bank_drained[t[0]], it * PER_TURN[t[0]] + written(t))
                    w2 = W[f"f2{b // 3}"]
                    for t in range(T4):
                        last = mm(bank(u, 0, D), hid[par][:, t, :], w2[:, t, :], start=(t == 0), stop=(t == T4 - 1))
                    last.then_inc(bank_full[u[0]], 1)
                elif step == "PJ":
                    t = UNIT[b, par, "PV"]
                    if fresh(pe, bank_drained[t[0]], written(t)):
                        pe.wait_ge(bank_drained[t[0]], it * PER_TURN[t[0]] + written(t))
                    wp = {3: W["proj1"], 4: W["out1"], 10: W["out3"]}.get(b)
                    mm(bank(u, 0, D), outT[par][:, :], wp[:, :] if wp is not None else c("ident"),
                            start=True, stop=True).then_inc(bank_full[u[0]], 1)

            set_up()
            first_par = {b: next(q for _, n, a, q in ORDER[PE] if (n, a) == ("T", b)) for b in range(LAST + 1)}
            with pe.Fori(0, PAIRS) as it:
                for _, step, b, par in ORDER[PE]:
                    step_of(it, step, b, par)

        @block.scalar
        def _(act):

            def set_up():
                act.wait_ge(small_loaded, 16 * 5)
                nc.scalar.activation(silu_t[:, 0:S], condT[:, :], ACT.Tanh, scale=0.5).then_inc(silu_in, 1)
                u = 1
                for n in ("sa0", "ca0", "sa2", "ca2"):
                    r = M[n].shape[0]
                    for g in range(4):
                        act.wait_ge(bank_full[u % BANKS], u // BANKS + 1)
                        nc.scalar.activation(M[n][:, g * BANK:(g + 1) * BANK], ps[0:r, u % BANKS, :], ACT.Copy)\
                          .then_inc(bank_drained[u % BANKS], 1)
                        u += 1

            def step_of(it, step, b, par):
                if step[:3] == "exp":
                    g = int(step[3])
                    u = UNIT[b, par, f"S{g}"]
                    count = AT["max", f"max{g}", b, par]
                    if fresh(act, signal["max"], count):
                        act.wait_ge(signal["max"], it * TOTAL["max"] + count)
                    for j in range(T4):
                        h = T4 * g + j
                        last = nc.scalar.activation(E[par][:, h, :], bank(u, j * N, (j + 1) * N), ACT.Exp,
                                                    bias=negmax[par][:, h:h + 1],
                                                    accum_out=sums[par][:, h:h + 1])
                    last.then_inc(bank_drained[u[0]], 1)
                    return
                u = UNIT[b, par, step]
                if fresh(act, bank_full[u[0]], written(u)):
                    act.wait_ge(bank_full[u[0]], it * PER_TURN[u[0]] + written(u))
                if step[:2] == "VW":
                    i = int(step[2])
                    nc.scalar.activation(VW[par][:, i * BANK:(i + 1) * BANK], bank(u), ACT.Copy).then_inc(bank_drained[u[0]], 1)
                elif step[:2] in ("QT", "KT"):
                    half = int(step[2])
                    dst = (qT if step[0] == "Q" else kT)[par]
                    nc.scalar.activation(dst[:, T4 * half:T4 * half + T4, :],
                                               bank(u).rearrange("p (t n) -> p t n", t=T4), ACT.Copy).then_inc(bank_drained[u[0]], 1)
                elif step == "Q":
                    for g in range(T4):
                        last = nc.scalar.activation(qT[par][:, g, :], bank(u, 0, N), ACT.Identity,
                                                    bias=qbias[b][:, g:g + 1] if b in qbias else 0.0,
                                                    scale=qscale[:, g:g + 1])
                    last.then_inc(bank_drained[u[0]], 1)
                elif b < L2_FF:
                    f, name = (ACT.Gelu, "ff1_0_") if b == 2 else (ACT.Gelu_apprx_tanh, "fc1_")
                    for t in range(T4):
                        last = nc.scalar.activation(hid[par][:, t, :], bank(u, t * N, (t + 1) * N), f,
                                                    bias=v(f"{name}{t}"))
                    last.then_inc(bank_drained[u[0]], 1)
                elif b == L2_FF:
                    for t in range(T4):
                        last = nc.scalar.activation(act_out[par][:, t, :], bank(u, t * N, (t + 1) * N), ACT.Gelu,
                                                    bias=v(f"ff1_2_{T4 + t}"))
                    last.then_inc(bank_drained[u[0]], 1)
                else:
                    nc.scalar.activation(act_out[par], bank(u).rearrange("p (t n) -> p t n", t=T4), ACT.Tanh,
                                         scale=0.5).then_inc(signal["tanh"], 1)

            set_up()
            act.wait_ge(q_constants, 1)
            with act.Fori(0, PAIRS) as it:
                for _, step, b, par in ORDER[ACTE]:
                    step_of(it, step, b, par)

        @block.gpsimd
        def _(pool):
            tt = nc.gpsimd.tensor_tensor

            def first_power(turn, par):
                for k in range(2):
                    pool.wait_ge(first["stats"][par], turn * 2 + (k + 1))
                    tt(rstd[par][:, k:k + 1], ve[par][:, k:k + 1], c("neghalf"), ALU.pow)\
                        .then_inc(first["power"][par], 1)

            def step_of(it, step, b, par):
                if step == "power" and b == 0:
                    first_power(it + 1, par)
                elif step == "power":
                    if fresh(pool, signal["stats"], AT["stats", "stats", b, par]):
                        pool.wait_ge(signal["stats"], it * TOTAL["stats"] + AT["stats", "stats", b, par])
                    tt(rstd[par][:, 0:1], ve[par][:, 0:1], c("neghalf"), ALU.pow).then_inc(signal["power"], 1)
                elif step[0] == "R":
                    n = step[1:]
                    m = ROPE.index((DVE, n, b, par))
                    t = UNIT[b, par, n]
                    if fresh(pool, bank_drained[t[0]], written(t)):
                        pool.wait_ge(bank_drained[t[0]], it * PER_TURN[t[0]] + written(t))
                    which, half = "QK".index(n[0]), int(n[1])
                    tt(rot[par][:, which, half * BANK:(half + 1) * BANK],
                       prod[:, m % 2, 0, :], prod[:, m % 2, 1, :], ALU.add).then_inc(signal["rotated"], 1)
                else:
                    g = int(step[4])
                    count = AT["rcp", f"rcp{g}", b, par]
                    if fresh(pool, signal["rcp"], count):
                        pool.wait_ge(signal["rcp"], it * TOTAL["rcp"] + count)
                    e = E[par][:, T4 * g:T4 * g + T4, :]
                    tt(e, e, rinv[par][:, T4 * g:T4 * g + T4].unsqueeze(2).broadcast_to([N, T4, N]),
                       ALU.mult).then_inc(signal["prob"], 1)

            pool.wait_ge(small_loaded, 16 * 5)
            for par in range(2):
                first_power(0, par)
            with pool.Fori(0, PAIRS) as it:
                for _, step, b, par in ORDER[POOL]:
                    step_of(it, step, b, par)

        @block.vector
        def _(dve):
            tt, ts = nc.vector.tensor_tensor, nc.vector.tensor_scalar
            steps = [0]
            loop = [0]

            def step(ins):
                ins.then_inc(dve_step, 1)
                steps[0] += 1
                return steps[0]

            def after(n):
                dve.wait_ge(dve_step, loop[0] * DVE_STEPS + n)

            def set_up():
                n = [0]

                def link(ins):
                    ins.then_inc(setup_step, 1)
                    n[0] += 1
                    dve.wait_ge(setup_step, n[0])

                dve.wait_ge(small_loaded, 16 * 5)
                dve.wait_ge(silu_in, 1)
                link(nc.vector.scalar_tensor_tensor(out=silu_t[:, S:2 * S], in0=silu_t[:, 0:S], scalar=1.0,
                                                    in1=condT[:, :], op0=ALU.add, op1=ALU.mult))
                ts(siluT[:, :], silu_t[:, S:2 * S], 0.5, None, ALU.mult).then_inc(silu_ready, 1)
                link(ts(qscale[:, :], c("groupmask"), float(HD) ** -0.5, None, ALU.mult))
                for dst, src in ((qbias[3][:, :], "bq1"), (qbias[10][:, :], "bq3"),
                                 (qn_masked[:, 0, :], "qn_w"), (qn_masked[:, 1, :], "qn_b")):
                    last = ts(dst, qscale[:, :], v(src), None, ALU.mult)
                last.then_inc(q_constants, 1)
                dve.wait_ge(bank_full[0], 1)
                last = tt(raw[:, :, :], ps[:, 0, 0:22 * S].rearrange("p (i s) -> p i s", s=S),
                          V[:, VEC["raw0"]:VEC["raw0"] + 22].unsqueeze(2).broadcast_to([128, 22, S]), ALU.add)
                last.then_inc(bank_drained[0], 1)
                dve.wait_ge(bank_drained[0], 1)
                for i in range(2):
                    g, s = raw[:, 2 * i, :], raw[:, 2 * i + 1, :]
                    lw, lb = v(f"ln{i + 1}_w"), v(f"ln{i + 1}_b")
                    link(ts(g, g, 1.0, None, ALU.add))
                    ts(mod[:, :, 2 * i], g, lw, None, ALU.mult)
                    link(ts(g, g, lb, None, ALU.mult))
                    link(tt(mod[:, :, 2 * i + 1], g, s, ALU.add))
                for j in range(2, NMOD):
                    scale, shift = (2 * j, 2 * j + 1) if 5 <= j < 8 else (2 * j + 1, 2 * j)
                    ts(mod[:, :, 2 * j], raw[:, scale, :], 1.0, None, ALU.add)
                    last = nc.vector.tensor_copy(mod[:, :, 2 * j + 1], raw[:, shift, :])
                link(last)

            def mods(it, par):
                nc.vector.tensor_copy(cb[par][:, :], siluT[:, bass.ds(it * 2 + par, 1)].broadcast_to([128, N]))
                after(step(nc.vector.tensor_copy(
                    modc[par][:, :], mod[:, bass.ds(it * 2 + par, 1), :].rearrange("p a m -> p (a m)"))))

            def first_stats(turn, par):
                dve.wait_ge(x_loaded[par], turn * 32 + 32)
                for i, src in enumerate((xin, cin)):
                    n = step(nc.vector.bn_stats(st[par][:, i, :], src[par][:, :]))
                after(n)
                step(tt(xb[par][:, :], xin[par][:, :], row(OUT_ROW[0]), ALU.add))
                for i in range(2):
                    n = step(nc.vector.bn_aggr(mv[par][:, i, :], st[par][:, i, :]))
                after(n)
                for i, eps in enumerate((EPS[0], EPS_CTX)):
                    ts(ve[par][:, i:i + 1], mv[par][:, i, 1:2], eps, None, ALU.add).then_inc(first["stats"][par], 1)

            def first_norm(turn, par):
                for i, (src, dst) in enumerate(((xin, xn), (cin, cn))):
                    dve.wait_ge(first["power"][par], turn * 2 + (i + 1))
                    ts(dst[par][:, :], src[par][:, :], mv[par][:, i, 0:1], rstd[par][:, i:i + 1],
                       ALU.subtract, ALU.mult).then_inc(first["norm"][par], 1)

            def stats(it, b, par):
                xt = X[par]
                after(step(nc.vector.bn_stats(st[par][:, 0, :], xt[:, :])))
                if b == L3_CROSS:
                    gated = step(tt(gb[par][:, :], gates[par][:, D:2 * D], row(OUT_ROW[b]), ALU.mult))
                elif OUT_ROW[b] is None:
                    step(nc.vector.tensor_copy(xb[par][:, :], xt[:, :]))
                else:
                    step(tt(xb[par][:, :], xt[:, :], row(OUT_ROW[b]), ALU.add))
                n = step(nc.vector.bn_aggr(mv[par][:, 0, :], st[par][:, 0, :]))
                if b == L3_CROSS:
                    after(gated)
                    n = step(tt(xb[par][:, :], xt[:, :], gb[par][:, :], ALU.add))
                after(n)
                ts(ve[par][:, 0:1], mv[par][:, 0, 1:2], EPS[b], None, ALU.add).then_inc(signal["stats"], 1)

            def norm(it, b, par):
                if fresh(dve, signal["power"], AT["power", "power", b, par]):
                    dve.wait_ge(signal["power"], it * TOTAL["power"] + AT["power", "power", b, par])
                ts(xn[par][:, :], X[par][:, :], mv[par][:, 0, 0:1], rstd[par][:, 0:1], ALU.subtract, ALU.mult)\
                    .then_inc(signal["norm"], 1)

            def heads(it, b, par):
                u = UNIT[b, par, "VAR"]
                if fresh(dve, bank_full[u[0]], written(u)):
                    dve.wait_ge(bank_full[u[0]], it * PER_TURN[u[0]] + written(u))
                ts(hve[par], bank(u, 0, N), EPS_HEAD, None, ALU.add).then_inc(bank_drained[u[0]], 1)
                if fresh(dve, bank_drained[u[0]], written(u)):
                    dve.wait_ge(bank_drained[u[0]], it * PER_TURN[u[0]] + written(u))
                y, a = hrs[par], hk[par]
                after(step(ts(a.bitcast(int32), hve[par].bitcast(int32), 1, None, ALU.logical_shift_right)))
                after(step(ts(y.bitcast(int32), a.bitcast(int32), -1.0, float(0x5F3759DF), ALU.mult, ALU.add)))
                for _ in range(3):
                    after(step(tt(a, y, y, ALU.mult)))
                    after(step(nc.vector.scalar_tensor_tensor(out=a, in0=a, scalar=-0.5, in1=hve[par],
                                                              op0=ALU.mult, op1=ALU.mult)))
                    after(step(nc.vector.scalar_tensor_tensor(out=y, in0=a, scalar=1.5, in1=y,
                                                              op0=ALU.add, op1=ALU.mult)))
                after(step(tt(hz[par], hc[par], y, ALU.mult)))
                for g in range(T4):
                    ts(qT[par][:, g, :], hz[par], qn_masked[:, 0, g:g + 1], qn_masked[:, 1, g:g + 1],
                       ALU.mult, ALU.add)
                after(step(ts(hk[par], hz[par], v("kn_w"), v("kn_b"), ALU.mult, ALU.add)))
                for j in range(T4):
                    last = ts(kT[par][:, j, :], hk[par], c("rowmask")[:, j:j + 1], None, ALU.mult)
                last.then_inc(signal["heads"], 1)

            def residual_sum(it, b, par):
                k = KIND[b]
                u = UNIT[b, par, "D" if k == "ff" else "PJ" if k == "small" else "PV"]
                if fresh(dve, bank_full[u[0]], written(u)):
                    dve.wait_ge(bank_full[u[0]], it * PER_TURN[u[0]] + written(u))
                if b == 0:
                    dve.wait_ge(ctxT_loaded[par], it * 16 + 16)
                if b < L3_SELF:
                    tt(X[par][:, :], bank(u, 0, D), xb[par][:, :], ALU.add).then_inc(bank_drained[u[0]], 1)
                    if fresh(dve, bank_drained[u[0]], written(u)):
                        dve.wait_ge(bank_drained[u[0]], it * PER_TURN[u[0]] + written(u))
                else:
                    i = b - L3_SELF
                    nc.vector.scalar_tensor_tensor(
                        out=res[par], in0=bank(u, 0, D), scalar=0.5 if b == L3_FF else 1.0,
                        in1=gates[par][:, i * D:(i + 1) * D], op0=ALU.mult, op1=ALU.mult).then_inc(bank_drained[u[0]], 1)
                    if fresh(dve, bank_drained[u[0]], written(u)):
                        dve.wait_ge(bank_drained[u[0]], it * PER_TURN[u[0]] + written(u))
                    ins = tt(X[par][:, :], res[par], xb[par][:, :], ALU.add)
                    if b == LAST:
                        ins.then_inc(out_ready[par], 1)
                    else:
                        after(step(ins))

            def read(it, n, b, par):
                k = KIND[b]
                u = UNIT[b, par, n]
                if n in ("Q0", "Q1", "K0", "K1") and k == "rope":
                    m = ROPE.index((DVE, n, b, par))
                    if m >= 2:
                        _, old, old_b, old_par = ROPE[m - 2]
                        count = AT["rotated", "R" + old, old_b, old_par]
                        if fresh(dve, signal["rotated"], count):
                            dve.wait_ge(signal["rotated"], it * TOTAL["rotated"] + count)
                if b == L3_FF and n == "U0":
                    count = AT["tanh", "U0", b, par]
                    if fresh(dve, signal["tanh"], count):
                        dve.wait_ge(signal["tanh"], it * TOTAL["tanh"] + count)
                else:
                    if fresh(dve, bank_full[u[0]], written(u)):
                        dve.wait_ge(bank_full[u[0]], it * PER_TURN[u[0]] + written(u))
                if n == "T":
                    m = 2 * MODPAIR[b]
                    ts(hT[par][:, :], bank(u, 0, N), modc[par][:, m:m + 1], modc[par][:, m + 1:m + 2],
                             ALU.mult, ALU.add).then_inc(bank_drained[u[0]], 1)
                elif n == "CT":
                    ts(kvT[par][0:CD, :], ps[0:CD, u[0], 0:N], LNC[:, 0:1], LNC[:, 1:2],
                             ALU.mult, ALU.add).then_inc(bank_drained[u[0]], 1)
                elif n == "C":
                    ts(kvT[par][:, :], bank(u, 0, N), v("bctx" if b == 4 else "bcond"), None, ALU.add).then_inc(bank_drained[u[0]], 1)
                elif n == "G":
                    tt(gates[par][:, :], bank(u, 0, 3 * D), row("g0", 3), ALU.add).then_inc(bank_drained[u[0]], 1)
                elif n in ("Q0", "Q1", "K0", "K1") and k == "rope":
                    q = bank(u).rearrange("p (h i e) -> p h i e", h=8, e=2)
                    cos, sin = (c("cosq"), c("sinq")) if n[0] == "Q" else (c("cosk"), c("sink"))
                    a = prod[:, m % 2, 0, :].rearrange("p (h i) -> p h i", h=8)
                    s = prod[:, m % 2, 1, :].rearrange("p (h i e) -> p h i e", h=8, e=2)
                    sn = sin.rearrange("p (i e) -> p i e", e=2)
                    tt(a, bank(u).rearrange("p (h i) -> p h i", h=8),
                       cos.unsqueeze(1).broadcast_to([128, 8, DH]), ALU.mult)
                    tt(s[:, :, :, 0], q[:, :, :, 1], sn[:, :, 0].unsqueeze(1).broadcast_to([128, 8, 32]), ALU.mult)
                    tt(s[:, :, :, 1], q[:, :, :, 0],
                             sn[:, :, 1].unsqueeze(1).broadcast_to([128, 8, 32]), ALU.mult).then_inc(bank_drained[u[0]], 1)
                elif n in ("Q0", "Q1", "K0", "K1"):
                    i = int(n[1])
                    src = bank(u).rearrange("p (t n) -> p t n", t=T4)
                    if n[0] == "Q":
                        ts(qT[par][:, T4 * i:T4 * i + T4, :], src, float(DH) ** -0.5, None, ALU.mult).then_inc(bank_drained[u[0]], 1)
                    else:
                        nc.vector.tensor_copy(kT[par][:, T4 * i:T4 * i + T4, :], src).then_inc(bank_drained[u[0]], 1)
                elif n == "K":
                    bk = {3: v("bk1"), 4: 0.0, 10: v("bk3")}[b]
                    for j in range(T4):
                        last = ts(kT[par][:, j, :], bank(u, 0, N), bk, c("rowmask")[:, j:j + 1], ALU.add, ALU.mult)
                    last.then_inc(bank_drained[u[0]], 1)
                elif n == "V":
                    bv = {3: row("bv1"), 10: row("bv3")}.get(b)
                    if bv is None:
                        nc.vector.tensor_copy(vb[par], bank(u, 0, D)).then_inc(bank_drained[u[0]], 1)
                    else:
                        tt(vb[par], bank(u, 0, D), bv, ALU.add).then_inc(bank_drained[u[0]], 1)
                    if fresh(dve, bank_drained[u[0]], written(u)):
                        dve.wait_ge(bank_drained[u[0]], it * PER_TURN[u[0]] + written(u))
                    tt(vmask[par], vb[par].unsqueeze(1).broadcast_to([N, T4, D]),
                       c("colmask").rearrange("p (j f) -> p j f", j=T4), ALU.mult).then_inc(signal["values"], 1)
                elif n == "HC":
                    nc.vector.tensor_copy(hc[par], bank(u, 0, N)).then_inc(bank_drained[u[0]], 1)
                    if fresh(dve, bank_drained[u[0]], written(u)):
                        dve.wait_ge(bank_drained[u[0]], it * PER_TURN[u[0]] + written(u))
                    tt(hsq[par], hc[par], hc[par], ALU.mult).then_inc(signal["squares"], 1)
                elif n[:2] == "PT":
                    g = int(n[2])
                    nc.vector.tensor_copy(PT[par][:, g * BANK:(g + 1) * BANK], bank(u)).then_inc(bank_drained[u[0]], 1)
                elif n == "PV":
                    nc.vector.tensor_copy(outT[par][:, :], bank(u, 0, N)).then_inc(bank_drained[u[0]], 1)
                elif b == L2_FF:
                    t = UNIT[b, par, "U1"]
                    if fresh(dve, bank_drained[t[0]], written(t)):
                        dve.wait_ge(bank_drained[t[0]], it * PER_TURN[t[0]] + written(t))
                    for t in range(T4):
                        last = nc.vector.scalar_tensor_tensor(
                            out=hid[par][:, t, :], in0=bank(u, t * N, (t + 1) * N), scalar=v(f"ff1_2_{t}"),
                            in1=act_out[par][:, t, :], op0=ALU.add, op1=ALU.mult)
                    last.then_inc(bank_drained[u[0]], 1)
                elif n == "U0":
                    nc.vector.scalar_tensor_tensor(
                        out=mid[par].rearrange("p t n -> p (t n)"), in0=act_out[par].rearrange("p t n -> p (t n)"),
                        scalar=1.0, in1=bank(u), op0=ALU.add, op1=ALU.mult).then_inc(bank_drained[u[0]], 1)
                else:
                    t = UNIT[b, par, "U0"]
                    if fresh(dve, bank_drained[t[0]], written(t)):
                        dve.wait_ge(bank_drained[t[0]], it * PER_TURN[t[0]] + written(t))
                    tt(hid[par].rearrange("p t n -> p (t n)"), mid[par].rearrange("p t n -> p (t n)"), bank(u),
                             ALU.mult).then_inc(bank_drained[u[0]], 1)

            def step_of(it, name, b, par):
                if name == "stats" and b == 0:
                    first_stats(it + 1, par)
                elif name == "stats":
                    stats(it, b, par)
                elif name == "norm" and b == 0:
                    first_norm(it + 1, par)
                elif name == "norm":
                    norm(it, b, par)
                elif name == "mods":
                    mods(it, par)
                elif name == "heads":
                    heads(it, b, par)
                elif name == "sum":
                    residual_sum(it, b, par)
                elif name[:3] == "max":
                    g = int(name[3])
                    u = UNIT[b, par, f"S{g}"]
                    if fresh(dve, bank_full[u[0]], written(u)):
                        dve.wait_ge(bank_full[u[0]], it * PER_TURN[u[0]] + written(u))
                    nc.vector.tensor_reduce(negmax[par][:, T4 * g:T4 * g + T4],
                                            bank(u).rearrange("p (h m) -> p h m", h=T4), AX, ALU.max,
                                            negate=True).then_inc(signal["max"], 1)
                elif name[:3] == "rcp":
                    g = int(name[3])
                    t = UNIT[b, par, f"S{g}"]
                    if fresh(dve, bank_drained[t[0]], written(t)):
                        dve.wait_ge(bank_drained[t[0]], it * PER_TURN[t[0]] + written(t))
                    hs = slice(T4 * g, T4 * g + T4)
                    nc.vector.reciprocal(rinv[par][:, hs], sums[par][:, hs]).then_inc(signal["rcp"], 1)
                else:
                    read(it, name, b, par)

            set_up()
            dve.wait_ge(q_constants, 1)
            for par in range(2):
                first_stats(0, par)
                first_norm(0, par)
            before_loop = steps[0]
            with dve.Fori(0, PAIRS) as it:
                loop[0] = it
                for _, name, b, par in ORDER[DVE]:
                    step_of(it, name, b, par)
            assert steps[0] - before_loop == DVE_STEPS, steps[0] - before_loop


def constants():
    t = np.zeros((128, NCONST), np.float32)
    p = np.arange(128)
    t[:, CONST["ident"]] = np.eye(128)
    mean8 = (p[:, None] // HD == p[None, :] // HD) / HD
    t[:, CONST["mean8"]] = mean8
    t[:, CONST["center"]] = np.eye(128) - mean8
    member = (p[:, None] // HD) % T4 == np.arange(T4)[None, :]
    t[:, CONST["rowmask"]] = member
    t[:, CONST["groupmask"]] = p[:, None] // 32 == np.arange(T4)[None, :]
    t[:, CONST["colmask"]] = member.T.reshape(1, -1)
    inv = (1.0 / np.float32(10000.0) ** (np.arange(0, DH, 2, dtype=np.float32) / np.float32(DH))).astype(np.float32)
    ang = np.arange(N, dtype=np.float32)[:, None] * inv[None, :]
    cos = np.repeat(np.cos(ang), 2, axis=1)
    sin = np.stack([-np.sin(ang), np.sin(ang)], axis=-1).reshape(N, DH)
    scale = float(DH) ** -0.5
    t[:, CONST["cosk"]], t[:, CONST["sink"]] = cos, sin
    t[:, CONST["cosq"]], t[:, CONST["sinq"]] = cos * scale, sin * scale
    t[:, CONST["neghalf"]] = -0.5
    return t


def laid_out(a):
    L0, L1, L2, L3 = ({k.removeprefix(f"L{i}_xcond_"): v for k, v in a.items() if k.startswith(f"L{i}_")}
                      for i in range(4))
    down = lambda m: m.reshape(T4, 128, D).transpose(1, 0, 2)
    ada_w, ada_b = L3["adaln_w"].reshape(9, D, D), L3["adaln_b"].reshape(9, D)
    plain, gate = [0, 1, 3, 4, 6, 7], [2, 5, 8]
    t16 = lambda v: np.tile(v, H)
    vecs = [L0["ln1_w"], L0["ln1_b"], L0["ln2_w"], L0["ln2_b"], L0["g1_b"], L0["b1_b"], L0["g2_b"], L0["b2_b"]]
    vecs += list(L1["b_ada"].reshape(6, D))
    for n in ("n1_b", "n2_b", "n3_b"):
        vecs += list(L2[n].reshape(2, D))
    vecs += [ada_b[i] for i in plain] + list(L0["ff_b1"].reshape(4, D))
    vecs += [L1["b_qkv"][0:D], L1["b_qkv"][D:2 * D], L1["b_ctx"]] + list(L1["b_fc1"].reshape(4, D))
    vecs += list(L2["ff_b1"].reshape(8, D))
    vecs += [t16(L3["qn_w"]), t16(L3["qn_b"]), t16(L3["kn_w"]), t16(L3["kn_b"])]
    vecs += [L3["ca_in_b"][0:D], L3["ca_in_b"][D:2 * D], L3["cond_b"]]
    rows = [L0["sa_bo"], L0["ca_bo"], L0["ff_b2"], L1["b_proj"], L1["b_out"], L1["b_fc2"],
            L2["o1_b"], L2["o2_b"], L2["ff_b2"], L3["ca_out_b"], L1["b_qkv"][2 * D:], L3["ca_in_b"][2 * D:]]
    rows += [ada_b[i] for i in gate]
    w = {"wq0": L0["sa_wq"], "wk0": L0["sa_wkv"][:, :MID], "cq0": L0["ca_wq"], "ck0": L0["ca_wkv"][:, :MID],
         "f10": L0["ff_w1"], "f20": down(L0["ff_w2"]),
         "qkv1": L1["W_qkv"], "proj1": L1["W_proj"], "ctx1": L1["W_ctx"],
         "cqkv1": np.concatenate([L1["W_q"], L1["W_k"], L1["W_v"]], axis=1), "out1": L1["W_out"],
         "f11": L1["W_fc1"], "f21": down(L1["W_fc2"]),
         "wq2": L2["q1"], "wk2": L2["k1"], "cq2": L2["q2"], "ck2": L2["k2"], "f12": L2["ff_w1"], "f22": down(L2["ff_w2"]),
         "gate3": np.concatenate([ada_w[i].T for i in gate], axis=1), "cond3": L3["cond_w"].T,
         "cqkv3": L3["ca_in_w"].T, "out3": L3["ca_out_w"].T,
         "f13": np.concatenate([L3["w1"].T, L3["w3"].T], axis=1), "f23": down(L3["w2"].T)}
    setup_w = {"vt_sa0": L0["sa_wkv"][:, MID:].T, "wo_sa0": L0["sa_wo"],
               "vt_ca0": L0["ca_wkv"][:, MID:].T, "wo_ca0": L0["ca_wo"],
               "vt_sa2": L2["v1"].T, "wo_sa2": L2["o1_w"], "vt_ca2": L2["v2"].T, "wo_ca2": L2["o2_w"],
               "mod_lin": np.concatenate([L0["g1_w"], L0["b1_w"], L0["g2_w"], L0["b2_w"],
                                          L2["n1_w"], L2["n2_w"], L2["n3_w"]], axis=1),
               "mod_silu": np.concatenate([L1["W_ada"]] + [ada_w[i].T for i in plain], axis=1)}
    main = {"x": a["x"], "ctx": a["ctx_768"], "ctx_t": a["ctx_768"].transpose(0, 2, 1), "cond_t": a["cond_1024"].T,
            "vecs": np.stack(vecs, axis=1), "lnc": np.stack([L0["ca_lnc_w"], L0["ca_lnc_b"]], axis=1),
            "rows": np.concatenate(rows), "consts": constants()}
    return main, setup_w, w


def kernel(**inputs):
    import concourse.bacc as bacc
    from concourse.bass_utils import run_bass_kernel_spmd

    nc = bacc.Bacc("TRN2", target_bir_lowering=False, num_devices=1)
    main, setup_w, w = laid_out({k: np.asarray(v) for k, v in inputs.items()})
    arrays = {}

    def declare(group, prefix):
        aps = {}
        for name, a in group.items():
            a = np.ascontiguousarray(a)
            arrays[prefix + name] = a
            aps[name] = nc.dram_tensor(prefix + name, a.shape, mybir.dt.from_np(a.dtype), kind="ExternalInput").ap()
        return aps

    m, s, r = declare(main, "in_"), declare(setup_w, "set_"), declare({n: w[n] for n in WEIGHTS}, "res_")
    out = nc.dram_tensor("out_x", (S, N, D), mybir.dt.float32, kind="ExternalOutput").ap()
    build(nc, m["x"], m["ctx"], m["ctx_t"], m["cond_t"], m["vecs"], m["lnc"], m["rows"], m["consts"], s, r, out)
    return run_bass_kernel_spmd(nc, [arrays], core_ids=[0]).results[0]["out_x"]
```
